# Optimizing a Trainium2 kernel written in Bass

```python
import numpy as np
import jax
import jax.numpy as jnp

def _softmax(x, axis=-1):
    return jax.nn.softmax(x, axis=axis)

def _gelu(x):
    return jax.nn.gelu(x, approximate=True)

def _silu(x):
    return jax.nn.silu(x)

def _sigmoid(x):
    return jax.nn.sigmoid(x)

def _layernorm(x, axis=-1, eps=1e-05):
    m = jnp.mean(x, axis=axis, keepdims=True)
    v = jnp.var(x, axis=axis, keepdims=True)
    return (x - m) / jnp.sqrt(v + eps)

def _scatter_add(tgt, idx, src, axis=0):
    return tgt.at[idx].add(src)

def _segment_sum(src, seg, n):
    return jax.ops.segment_sum(src, seg, n)
kernel_name = 'mk_sandwich_d1_jaxref_r8_e53ea6'

def setup_inputs(seed: int=0):
    np.random.seed(seed)
    _w = jnp.asarray

    def _L0_attn_setup():
        import jax, jax.numpy as jnp
        import numpy as np
        B, T, D = (2, 512, 128)
        H, DK, DV, K = (16, 64, 128, 4)
        EPS = 1e-06

        def _causal_conv_silu(x, w):
            Kw = w.shape[1]
            xp = jnp.pad(x, ((0, 0), (Kw - 1, 0), (0, 0)))
            y = sum((w[:, j] * xp[:, j:j + x.shape[1], :] for j in range(Kw)))
            return jax.nn.silu(y)

        def _l2_norm(x, eps=EPS):
            n = jnp.sqrt(jnp.sum(x * x, axis=-1, keepdims=True))
            return x / jnp.maximum(n, eps)

        def _rms_norm(x, eps=EPS):
            x32 = x.astype(jnp.float32)
            ms = jnp.mean(x32 * x32, axis=-1, keepdims=True)
            return x32 * jax.lax.rsqrt(ms + eps)

        def _gdn_recurrence(q, k, v, alpha, beta):

            def step(S, inp):
                q_t, k_t, v_t, a_t, b_t = inp
                kS = jnp.einsum('bhd,bhdv->bhv', k_t, S)
                kkS = jnp.einsum('bhd,bhv->bhdv', k_t, kS)
                S = a_t[..., None, None] * (S - b_t[..., None, None] * kkS) + jnp.einsum('bhd,bhv->bhdv', k_t, v_t)
                o_t = jnp.einsum('bhdv,bhd->bhv', S, q_t)
                return (S, o_t)
            S0 = jnp.zeros((q.shape[0], H, DK, DV), dtype=jnp.float32)
            tm = lambda a: jnp.moveaxis(a, 1, 0)
            S, o = jax.lax.scan(step, S0, (tm(q), tm(k), tm(v), tm(alpha), tm(beta)))
            return (jnp.moveaxis(o, 0, 1), S)
        key = jax.random.key(seed)
        ks = jax.random.split(key, 13)
        s = lambda d: 1.0 / np.sqrt(d)
        inp = {'x': jax.random.normal(ks[0], (B, T, D), dtype=jnp.float32), 'Wq': jax.random.normal(ks[1], (H * DK, D), dtype=jnp.float32) * s(D), 'Wk': jax.random.normal(ks[2], (H * DK, D), dtype=jnp.float32) * s(D), 'Wv': jax.random.normal(ks[3], (H * DV, D), dtype=jnp.float32) * s(D), 'Wb': jax.random.normal(ks[4], (H, D), dtype=jnp.float32) * s(D), 'Wa': jax.random.normal(ks[5], (H, D), dtype=jnp.float32) * s(D), 'A_log': jax.random.normal(ks[6], (H,), dtype=jnp.float32) * 0.5, 'dt_bias': jax.random.normal(ks[7], (H,), dtype=jnp.float32) * 0.5, 'Wo': jax.random.normal(ks[8], (D, H * DV), dtype=jnp.float32) * s(H * DV), 'conv_q': jax.random.normal(ks[9], (H * DK, K), dtype=jnp.float32) * s(K), 'conv_k': jax.random.normal(ks[10], (H * DK, K), dtype=jnp.float32) * s(K), 'conv_v': jax.random.normal(ks[11], (H * DV, K), dtype=jnp.float32) * s(K)}
        return inp
    _L0_attn_in = _L0_attn_setup()

    def _L0_ffn_setup():
        import jax, jax.numpy as jnp
        import numpy as np
        DIM = 128

        def _reference_tuple_inner(x, W_r, W_k, W_v, mu_r, mu_k):
            B, T, C = x.shape
            x_prev = jnp.concatenate([jnp.zeros((B, 1, C), x.dtype), x[:, :-1, :]], axis=1)
            xr = mu_r * x + (1.0 - mu_r) * x_prev
            xk = mu_k * x + (1.0 - mu_k) * x_prev
            r = jax.nn.sigmoid(jnp.einsum('btc,dc->btd', xr, W_r))
            k = jnp.einsum('btc,dc->btd', xk, W_k)
            k_act = jnp.square(jax.nn.relu(k))
            out = r * jnp.einsum('btc,dc->btd', k_act, W_v)
            new_state = x[:, -1, :]
            return (out, new_state)
        key = jax.random.key(seed)
        ks = jax.random.split(key, 6)
        B, T, C = (8, 256, DIM)
        x = jax.random.normal(ks[0], (B, T, C), dtype=jnp.float32)
        s = 1.0 / np.sqrt(C)
        W_r = jax.random.uniform(ks[1], (C, C), jnp.float32, -s, s)
        W_k = jax.random.uniform(ks[2], (C, C), jnp.float32, -s, s)
        W_v = jax.random.uniform(ks[3], (C, C), jnp.float32, -s, s)
        mu_r = jax.random.uniform(ks[4], (C,), jnp.float32)
        mu_k = jax.random.uniform(ks[5], (C,), jnp.float32)
        return {'x': x, 'W_r': W_r, 'W_k': W_k, 'W_v': W_v, 'mu_r': mu_r, 'mu_k': mu_k}
    _L0_ffn_in = _L0_ffn_setup()
    _d = {'L0_attn_x': _L0_attn_in['x'], 'L0_attn_Wq': _L0_attn_in['Wq'], 'L0_attn_Wk': _L0_attn_in['Wk'], 'L0_attn_Wv': _L0_attn_in['Wv'], 'L0_attn_Wb': _L0_attn_in['Wb'], 'L0_attn_Wa': _L0_attn_in['Wa'], 'L0_attn_A_log': _L0_attn_in['A_log'], 'L0_attn_dt_bias': _L0_attn_in['dt_bias'], 'L0_attn_Wo': _L0_attn_in['Wo'], 'L0_attn_conv_q': _L0_attn_in['conv_q'], 'L0_attn_conv_k': _L0_attn_in['conv_k'], 'L0_attn_conv_v': _L0_attn_in['conv_v'], 'L0_ffn_W_r': _L0_ffn_in['W_r'], 'L0_ffn_W_k': _L0_ffn_in['W_k'], 'L0_ffn_W_v': _L0_ffn_in['W_v'], 'L0_ffn_mu_r': _L0_ffn_in['mu_r'], 'L0_ffn_mu_k': _L0_ffn_in['mu_k']}
    _x0 = _d['L0_attn_x']
    _d['L0_attn_x'] = jax.random.normal(jax.random.fold_in(jax.random.key(seed), 1), (8, 1024, 128), dtype=_x0.dtype)
    del _x0
    return _d

def reference(L0_attn_x, L0_attn_Wq, L0_attn_Wk, L0_attn_Wv, L0_attn_Wb, L0_attn_Wa, L0_attn_A_log, L0_attn_dt_bias, L0_attn_Wo, L0_attn_conv_q, L0_attn_conv_k, L0_attn_conv_v, L0_ffn_W_r, L0_ffn_W_k, L0_ffn_W_v, L0_ffn_mu_r, L0_ffn_mu_k):

    def _L0_attn_ref(x, Wq, Wk, Wv, Wb, Wa, A_log, dt_bias, Wo, conv_q, conv_k, conv_v):
        import jax, jax.numpy as jnp
        import numpy as np
        B, T, D = (2, 512, 128)
        H, DK, DV, K = (16, 64, 128, 4)
        EPS = 1e-06

        def _causal_conv_silu(x, w):
            Kw = w.shape[1]
            xp = jnp.pad(x, ((0, 0), (Kw - 1, 0), (0, 0)))
            y = sum((w[:, j] * xp[:, j:j + x.shape[1], :] for j in range(Kw)))
            return jax.nn.silu(y)

        def _l2_norm(x, eps=EPS):
            n = jnp.sqrt(jnp.sum(x * x, axis=-1, keepdims=True))
            return x / jnp.maximum(n, eps)

        def _rms_norm(x, eps=EPS):
            x32 = x.astype(jnp.float32)
            ms = jnp.mean(x32 * x32, axis=-1, keepdims=True)
            return x32 * jax.lax.rsqrt(ms + eps)

        def _gdn_recurrence(q, k, v, alpha, beta):

            def step(S, inp):
                q_t, k_t, v_t, a_t, b_t = inp
                kS = jnp.einsum('bhd,bhdv->bhv', k_t, S)
                kkS = jnp.einsum('bhd,bhv->bhdv', k_t, kS)
                S = a_t[..., None, None] * (S - b_t[..., None, None] * kkS) + jnp.einsum('bhd,bhv->bhdv', k_t, v_t)
                o_t = jnp.einsum('bhdv,bhd->bhv', S, q_t)
                return (S, o_t)
            S0 = jnp.zeros((q.shape[0], H, DK, DV), dtype=jnp.float32)
            tm = lambda a: jnp.moveaxis(a, 1, 0)
            S, o = jax.lax.scan(step, S0, (tm(q), tm(k), tm(v), tm(alpha), tm(beta)))
            return (jnp.moveaxis(o, 0, 1), S)
        Bx, Tx = (x.shape[0], x.shape[1])
        q = _causal_conv_silu(x @ Wq.T, conv_q).reshape(Bx, Tx, H, DK)
        k = _causal_conv_silu(x @ Wk.T, conv_k).reshape(Bx, Tx, H, DK)
        v = _causal_conv_silu(x @ Wv.T, conv_v).reshape(Bx, Tx, H, DV)
        q = _l2_norm(q)
        k = _l2_norm(k)
        a_lin = (x @ Wa.T).astype(jnp.float32)
        alpha = jnp.exp(-jnp.exp(A_log) * jax.nn.softplus(a_lin + dt_bias))
        beta = 2.0 * jax.nn.sigmoid(x @ Wb.T)
        o, _S = _gdn_recurrence(q.astype(jnp.float32), k.astype(jnp.float32), v.astype(jnp.float32), alpha, beta)
        o = _rms_norm(o).astype(x.dtype).reshape(Bx, Tx, H * DV)
        return o @ Wo.T

    def _L0_ffn_ref(x, W_r, W_k, W_v, mu_r, mu_k):
        import jax, jax.numpy as jnp
        import numpy as np
        DIM = 128

        def _reference_tuple_inner(x, W_r, W_k, W_v, mu_r, mu_k):
            B, T, C = x.shape
            x_prev = jnp.concatenate([jnp.zeros((B, 1, C), x.dtype), x[:, :-1, :]], axis=1)
            xr = mu_r * x + (1.0 - mu_r) * x_prev
            xk = mu_k * x + (1.0 - mu_k) * x_prev
            r = jax.nn.sigmoid(jnp.einsum('btc,dc->btd', xr, W_r))
            k = jnp.einsum('btc,dc->btd', xk, W_k)
            k_act = jnp.square(jax.nn.relu(k))
            out = r * jnp.einsum('btc,dc->btd', k_act, W_v)
            new_state = x[:, -1, :]
            return (out, new_state)
        return _reference_tuple_inner(x, W_r, W_k, W_v, mu_r, mu_k)[0]
    x = L0_attn_x
    x = x + _layernorm(_L0_attn_ref(_layernorm(x, axis=-1), L0_attn_Wq, L0_attn_Wk, L0_attn_Wv, L0_attn_Wb, L0_attn_Wa, L0_attn_A_log, L0_attn_dt_bias, L0_attn_Wo, L0_attn_conv_q, L0_attn_conv_k, L0_attn_conv_v), axis=-1)
    x = x + _layernorm(_L0_ffn_ref(_layernorm(x, axis=-1), L0_ffn_W_r, L0_ffn_W_k, L0_ffn_W_v, L0_ffn_mu_r, L0_ffn_mu_k), axis=-1)
    return x

_drawn_inputs = setup_inputs


def setup_inputs(seed=0):
    import zlib

    import numpy as np

    out = dict(_drawn_inputs(seed))
    spreads = {}
    factors = {}
    for name, (base, spread) in spreads.items():
        noise = np.random.default_rng([zlib.crc32(name.encode()), seed]).standard_normal(out[name].shape)
        drawn = base * np.exp(spread * noise) if base else spread * noise
        out[name] = jnp.asarray(drawn.astype(out[name].dtype))
    for name, factor in factors.items():
        out[name] = (out[name] * factor).astype(out[name].dtype)
    return out
```

```python
import numpy as np
import concourse.bass as bass
from concourse import mybir
from contextlib import ExitStack

F32 = mybir.dt.float32
U32 = mybir.dt.uint32
ALU = mybir.AluOpType
ACT = mybir.ActivationFunctionType

P = 128
NB = 8
T = 1024
D = 128
H = 16
HP = H // 2
DK = 64
DV = 128
C = 64
NC = T // C
STEPS = HP * NC
TAPS = 4
HALO = TAPS - 1
CW = C + HALO
NT = T // P
LEVELS = 6
HALF = ((0, 64), (64, 128))
RESET = -1.0e4
EPS_LN = 1e-5
EPS_L2 = 1e-6
EPS_RMS = 1e-6

K_ID, K_LE, K_GT, K_BD, K_ONE, K_MGT, K_MLE, K_NEG, K_LV = 0, 128, 256, 384, 512, 640, 704, 768, 832
K_N = K_LV + LEVELS * P


def constants():
    c = np.zeros((P, K_N), np.float32)
    i = np.arange(P)
    same = (i[:, None] // C) == (i[None, :] // C)
    r, t = (i % C)[:, None], (i % C)[None, :]
    c[:, K_ID:K_ID + P] = np.eye(P)
    c[:, K_LE:K_LE + P] = same & (r <= t)
    c[:, K_GT:K_GT + P] = same & (r > t)
    c[:, K_BD:K_BD + P] = same
    c[:, K_ONE:K_ONE + P] = 1.0 / DV
    j = np.arange(C)[None, :]
    c[:, K_MGT:K_MGT + C] = r > j
    c[:, K_MLE:K_MLE + C] = r <= j
    c[:, K_NEG:K_NEG + C] = -1.0 * (r > j)
    for lv in range(LEVELS):
        n = 1 << lv
        c[:, K_LV + lv * P:K_LV + (lv + 1) * P] = same & (r // n % 2 == 0) & (t // n == r // n + 1)
    return c


class Signal:

    def __init__(self, sem, per):
        self.sem, self.per = sem, per

    def at(self, step, k=None):
        return step * self.per + (self.per if k is None else k)


def build(nc, x, wtab, wo, wab, hcol, cst, wf, mu, out):
    with ExitStack() as ctx:
        def sb(name, cols, dt=F32):
            return ctx.enter_context(nc.sbuf_tensor(name, [P, cols], dt))

        def sig(name, per=1):
            return Signal(ctx.enter_context(nc.semaphore(name)), per)

        k_all = sb("k_all", K_N)
        xnT = sb("xnT", NB * (HALO + T))
        accT = sb("accT", NB * T)
        tabP = sb("tabP", STEPS * 24)
        tabR = sb("tabR", STEPS * 16)
        xnT3 = xnT[:].rearrange("p (b t) -> p b t", b=NB)
        accT3 = accT[:].rearrange("p (b t) -> p b t", b=NB)
        w_s = sb("w_s", 4 * P + 16)
        wo_s = sb("wo_s", 2 * D)
        stP = sb("stP", 24)
        stR = sb("stR", 16)
        Lm = sb("Lm", 2 * 512)
        ex = sb("ex", 3 * 512)
        cv = sb("cv", 4 * 512)
        sl = sb("sl", 2 * 512)
        sv = sb("sv", 1024)
        sq = sb("sq", 2 * 512)
        rn = sb("rn", 2 * 512)
        qn = sb("qn", 512)
        BD = {n: sb(n, NB * P) for n in ("KB", "QG", "PT", "NM", "Z", "X", "Y", "KT")}
        Vt = sb("Vt", NB * P)
        Rr = sb("Rr", NB * P)
        U = sb("U", NB * P)
        S = sb("S", NB * P)
        osq = sb("osq", 1024)
        orn = sb("orn", 1024)
        on = sb("on", 1024)
        eps = sb("eps", 2)
        small = sb("small", 256)
        hc = sb("hc", 16)
        muc = sb("muc", 2)

        def bd(n):
            return BD[n][:].rearrange("p (b c) -> p b c", b=NB)

        ps = ctx.enter_context(nc.psum_tensor("ps", [P, 8 * 512], F32))

        def bank(i, n=1):
            return ps[:, i * 512:(i + n) * 512]

        def kc(o, n=P):
            return k_all[:, o:o + n]

        ident = kc(K_ID)

        def bcast(ap, n):
            return ap.rearrange("p (b o) -> p b o", o=1).to_broadcast([P, NB, n])

        def over(ap, b, n):
            return ap.rearrange("p (o n) -> p o n", o=1).to_broadcast([P, b, n])

        c_in = sig("c_in")
        x_in = [sig("x_in0"), sig("x_in1")]
        x_free = sig("x_free")
        zeroed = sig("zeroed")
        stats = sig("stats")
        rstd_s = sig("rstd_s")
        rstd_v = sig("rstd_v")
        xn_ok = sig("xn_ok")
        xn_tr = sig("xn_tr")
        xn_ev = sig("xn_ev")
        dchain = sig("dchain")
        lin = sig("lin")
        zz = sig("zz")
        a_step = sig("a_step")
        v_step = sig("v_step")
        cum = sig("cum")
        cexp = sig("cexp")

        xt = [KBuf for KBuf in (BD["KB"], BD["QG"])]
        xn = [BD["PT"], BD["NM"]]
        wab_s = cv[:, 0:32]
        la = Vt
        be = Rr
        tmp = [U, S, osq]
        x_tok = x.rearrange("b (j p) d -> b p j d", p=P)
        pairs = [(b // 2, b % 2) for b in range(NB)]

        with nc.Block() as block:
            @block.sync
            def _(sp):
                sp.dma_start(k_all[:], cst).then_inc(c_in.sem, 16)
                sp.dma_start(wab_s, wab).then_inc(c_in.sem, 16)
                sp.dma_start(hc[:], hcol).then_inc(c_in.sem, 16)
                sp.dma_start(muc[:], mu).then_inc(c_in.sem, 16)
                for b in range(NB):
                    if b >= 2:
                        sp.wait_ge(x_free.sem, b - 1)
                    sp.dma_start(xt[b % 2][:].rearrange("p (j d) -> p j d", j=NT), x_tok[b]).then_inc(x_in[b % 2].sem, 16)

            @block.gpsimd
            def _(pool):
                nc.gpsimd.memset(eps[:, 0:1], EPS_LN).then_inc(zeroed.sem, 1)
                nc.gpsimd.memset(eps[:, 1:2], EPS_RMS).then_inc(zeroed.sem, 1)
                nc.gpsimd.memset(xnT3[:, :, 0:HALO], 0.0).then_inc(zeroed.sem, 1)
                nc.gpsimd.memset(accT[:], 0.0).then_inc(zeroed.sem, 1)

            @block.vector
            def _(dve):
                chain = [0]

                def then(ins):
                    chain[0] += 1
                    ins.then_inc(dchain.sem, 1)
                    dve.wait_ge(dchain.sem, chain[0])

                for b in range(NB):
                    src = xt[b % 2][:].rearrange("p (j d) -> p j d", j=NT)
                    dst = xn[b % 2][:].rearrange("p (j d) -> p j d", j=NT)
                    dve.wait_ge(x_in[b % 2].sem, 16 * (b // 2 + 1))
                    st = small[:, 0:6 * NT].rearrange("p (j k) -> p j k", j=NT)
                    ag = small[:, 64:64 + 2 * NT].rearrange("p (j k) -> p j k", j=NT)
                    for j in range(NT):
                        last = nc.vector.bn_stats(st[:, j, :], src[:, j, :])
                    then(last)
                    for j in range(NT):
                        last = nc.vector.bn_aggr(ag[:, j, :], st[:, j, :])
                    last.then_inc(stats.sem, 1)
                    dve.wait_ge(rstd_s.sem, b + 1)
                    then(nc.vector.reciprocal(small[:, 96:96 + NT], small[:, 88:88 + NT]))
                    if b >= 2:
                        dve.wait_ge(xn_tr.sem, b - 1)
                    for j in range(NT):
                        last = nc.vector.tensor_scalar(dst[:, j, :], src[:, j, :], ag[:, j, 0:1], small[:, 96 + j:97 + j],
                                                       ALU.subtract, ALU.mult)
                        if j == NT - 1:
                            last.then_inc(xn_ok.sem, 1)
                    dve.wait_ge(xn_ok.sem, b + 1)
                    dve.sem_inc(x_free.sem, 1)
                dve.wait_ge(lin.sem, 1)
                raw = bank(0, 4).rearrange("p (n k) -> p n k", k=16)
                for hp in range(HP):
                    nc.vector.tensor_scalar(la[:, hp * P:(hp + 1) * P], raw[:, :, hp], hc[:, hp:hp + 1], None, ALU.add)
                    last = nc.vector.tensor_copy(be[:, hp * P:(hp + 1) * P], raw[:, :, 8 + hp])
                last.then_inc(zz.sem, 1)
                dve.wait_ge(zz.sem, 1)
                then(nc.vector.tensor_scalar(tmp[0][:], la[:], 0.0, None, ALU.max))
                dve.wait_ge(a_step.sem, 1)
                then(nc.vector.tensor_tensor(tmp[0][:], tmp[0][:], tmp[1][:], ALU.add))
                for hp in range(HP):
                    last = nc.vector.tensor_scalar(la[:, hp * P:(hp + 1) * P], tmp[0][:, hp * P:(hp + 1) * P],
                                                   hc[:, 8 + hp:9 + hp], -1.0, ALU.mult, ALU.mult)
                then(last)
                la4 = la[:].rearrange("p (h c b) -> p h c b", h=HP, c=NC)
                nc.vector.memset(la4[0:1, :, 0, :], RESET)
                then(nc.vector.memset(la4[64:65, :, 0, :], RESET))
                dve.sem_inc(v_step.sem, 1)
                then(nc.vector.tensor_scalar(be[:], be[:], 1.0, None, ALU.add))
                then(nc.vector.reciprocal(tmp[1][:], be[:]))
                then(nc.vector.tensor_scalar(be[:], tmp[1][:], 2.0, None, ALU.mult))
                tp = tabP[:].rearrange("p (n k) -> p n k", k=24)
                tr = tabR[:].rearrange("p (n k) -> p n k", k=16)
                v8 = lambda t: t[:].rearrange("p (n k) -> p n k", k=8)
                nc.vector.tensor_copy(tp[:, :, 0:8], v8(la))
                nc.vector.tensor_copy(tp[:, :, 8:16], v8(be))
                dve.wait_ge(cexp.sem, 1)
                nc.vector.scalar_tensor_tensor(tr[:, :, 0:8], v8(tmp[0]), -1.0, v8(be), ALU.mult, ALU.mult)
                then(nc.vector.memset(S[:], 0.0))
                for n in BD:
                    last = nc.vector.memset(BD[n][:], 0.0)
                then(last)

            @block.scalar
            def _(act):
                act.wait_ge(zeroed.sem, 4)
                for b in range(NB):
                    act.wait_ge(stats.sem, b + 1)
                    ag = small[:, 64:64 + 2 * NT].rearrange("p (j k) -> p j k", j=NT)
                    nc.scalar.activation(small[:, 88:88 + NT], ag[:, :, 1], ACT.Sqrt, bias=eps[:, 0:1]).then_inc(rstd_s.sem, 1)
                    act.wait_ge(xn_tr.sem, b + 1)
                    nc.scalar.activation(xnT3[:, b, HALO:HALO + T], bank(2 * (b % 2), 2), ACT.Copy).then_inc(xn_ev.sem, 1)
                act.preload_act_table_set("natural_log_exp_and_others")
                act.wait_ge(zz.sem, 1)
                steps = [0]

                def then(ins):
                    steps[0] += 1
                    ins.then_inc(rstd_v.sem, 1)
                    act.wait_ge(rstd_v.sem, steps[0])

                then(nc.scalar.activation(tmp[1][:], la[:], ACT.Abs))
                then(nc.scalar.activation(tmp[1][:], tmp[1][:], ACT.Exp, scale=-1.0))
                then(nc.scalar.activation(tmp[1][:], tmp[1][:], ACT.Ln, bias=1.0))
                then(nc.scalar.activation(hc[:, 8:16], hc[:, 8:16], ACT.Exp))
                nc.scalar.activation(be[:], be[:], ACT.Exp, scale=-1.0).then_inc(a_step.sem, 1)
                tp = tabP[:].rearrange("p (n k) -> p n k", k=24)
                tr = tabR[:].rearrange("p (n k) -> p n k", k=16)
                p8 = lambda i: bank(i, 2).rearrange("p (n k) -> p n k", k=8)
                act.wait_ge(cum.sem, 1)
                nc.scalar.activation(tmp[0][:], bank(0, 2), ACT.Exp).then_inc(cexp.sem, 1)
                nc.scalar.activation(tp[:, :, 16:24], p8(2), ACT.Exp)
                nc.scalar.activation(tr[:, :, 8:16], p8(4), ACT.Exp).then_inc(cexp.sem, 1)

            @block.tensor
            def _(pe):
                pe.wait_ge(c_in.sem, 64)
                for b in range(NB):
                    pe.wait_ge(xn_ok.sem, b + 1)
                    if b >= 2:
                        pe.wait_ge(xn_ev.sem, b - 1)
                    for j in range(NT):
                        last = nc.tensor.transpose(ps[:, (b % 2) * 1024 + j * P:(b % 2) * 1024 + (j + 1) * P],
                                                   xn[b % 2][:, j * P:(j + 1) * P], ident)
                    last.then_inc(xn_tr.sem, 1)
                pe.wait_ge(xn_ev.sem, NB)
                for c in range(NC):
                    for b in range(NB):
                        for h in range(2):
                            o = (c * NB + b) * 16
                            last = nc.tensor.matmul(ps[64 * h:64 * h + 64, o:o + 16], xnT3[:, b, HALO + c * C:HALO + (c + 1) * C],
                                                    wab_s[:, 16 * h:16 * h + 16], start=True, stop=True)
                last.then_inc(lin.sem, 1)
                pe.wait_ge(v_step.sem, 1)
                for i, o in enumerate((K_LE, K_GT, K_BD)):
                    for k in range(2):
                        last = nc.tensor.matmul(bank(2 * i + k), kc(o), la[:, k * 512:(k + 1) * 512], start=True, stop=True)
                last.then_inc(cum.sem, 1)

        w_in = sig("w_in", 16)
        st_ok = sig("st_ok")
        lm_ok = sig("lm_ok", 2)
        dec_mm = sig("dec_mm", 3)
        dec_ex = sig("dec_ex", 3)
        dmul = sig("dmul", 3)
        proj = sig("proj", 4)
        tap0 = sig("tap0", 4)
        conv = sig("conv", 12)
        silu = sig("silu", 4)
        sqr = sig("sqr", 2)
        nrm_mm = sig("nrm_mm", 2)
        nrm_mx = sig("nrm_mx", 2)
        nrm_ln = sig("nrm_ln", 2)
        nrm_rn = sig("nrm_rn", 2)
        kb_ok = sig("kb_ok")
        qn_ok = sig("qn_ok")
        qg_ok = sig("qg_ok", 2)
        gram_k = sig("gram_k", 2)
        gram_p = sig("gram_p")
        nm_ok = sig("nm_ok", 2)
        pt_ok = sig("pt_ok")
        z_one = sig("z_one")
        y_mm = sig("y_mm", 10)
        y_ok = sig("y_ok", 10)
        z_mm = sig("z_mm", 12)
        z_go = sig("z_go", 12)
        z_ok = sig("z_ok", 12)
        x_mm = sig("x_mm", 10)
        x_ok = sig("x_ok", 10)
        v_tr = sig("v_tr")
        v_ok = sig("v_ok")
        k_tr = sig("k_tr")
        kt_ok = sig("kt_ok")
        wo_in = sig("wo_in", 16)
        stR_ok = sig("stR_ok")
        ks_mm = sig("ks_mm", 2)
        r_ok = sig("r_ok", 2)
        u_mm = sig("u_mm", 2)
        u_ok = sig("u_ok", 2)
        o_mm = sig("o_mm", 2)
        ds_mm = sig("ds_mm", 2)
        s_ok = sig("s_ok", 2)
        o_sq = sig("o_sq", 2)
        ms_mm = sig("ms_mm", 2)
        ms_ln = sig("ms_ln", 2)
        ms_rn = sig("ms_rn", 2)
        on_ok = sig("on_ok", 2)
        wo_mm = sig("wo_mm")
        acc_ok = sig("acc_ok")

        tabP3 = tabP[:].rearrange("p (n k) -> p n k", k=24)
        tabR3 = tabR[:].rearrange("p (n k) -> p n k", k=16)
        cv4 = cv[:].rearrange("p (i b t) -> p i b t", i=4, b=NB)
        sv4 = sv[:].rearrange("p (b h t) -> p b h t", b=NB, h=2)
        v3 = lambda t, i: t[:, i * 512:(i + 1) * 512].rearrange("p (b t) -> p b t", b=NB)
        pj = bank(0, 2).rearrange("p (b t) -> p b t", b=NB)
        unit = lambda t, b: t[:, b * P:(b + 1) * P]
        LMASK = [k_all[:, K_LV + lv * P:K_LV + (lv + 1) * P].bitcast(U32) for lv in range(LEVELS)]
        GROUPS = (range(0, 4), range(4, 8))

        def pe_proj(pe, n, j):
            if j == 0:
                pe.wait_ge(w_in.sem, w_in.at(n))
                pe.wait_ge(xn_ev.sem, NB)
                if not first(n):
                    pe.wait_ge(kt_ok.sem, kt_ok.at(n - 1))
            else:
                pe.wait_ge(conv.sem, conv.at(n, 3 * j))
            for g in range(2):
                base = (n % NC) * C
                last = nc.tensor.matmul(pj[:, 4 * g:4 * g + 4, 0:CW], w_s[:, j * P:(j + 1) * P],
                                        xnT3[:, 4 * g:4 * g + 4, bass.ds(base, CW)], start=True, stop=True)
            last.then_inc(proj.sem, 1)

        def first(n):
            return isinstance(n, int) and n == 0

        def pe_decay(pe, n):
            if not first(n):
                pe.wait_ge(z_ok.sem, z_ok.at(n - 1))
                pe.wait_ge(x_ok.sem, x_ok.at(n - 1))
                pe.wait_ge(y_ok.sem, y_ok.at(n - 1))
            pe.wait_ge(lm_ok.sem, lm_ok.at(n, 1))
            nc.tensor.matmul(bank(2), kc(K_LE), Lm[:, 0:512], start=True, stop=True).then_inc(dec_mm.sem, 1)
            pe.wait_ge(lm_ok.sem, lm_ok.at(n, 2))
            nc.tensor.matmul(bank(3), kc(K_GT), Lm[:, 512:1024], start=True, stop=True).then_inc(dec_mm.sem, 1)

        def pe_decay_g(pe, n):
            pe.wait_ge(dec_ex.sem, dec_ex.at(n, 1))
            nc.tensor.matmul(bank(2), kc(K_BD), Lm[:, 512:1024], start=True, stop=True).then_inc(dec_mm.sem, 1)

        def pe_norm(pe, n, i):
            pe.wait_ge(sqr.sem, sqr.at(n, i + 1))
            pe.wait_ge(dec_ex.sem, dec_ex.at(n, 2 if i == 0 else 3))
            nc.tensor.matmul(bank(3 - i), kc(K_BD), sq[:, i * 512:(i + 1) * 512], start=True, stop=True).then_inc(nrm_mm.sem, 1)

        def pe_gram(pe, n):
            pe.wait_ge(kb_ok.sem, kb_ok.at(n))
            pe.wait_ge(nrm_mx.sem, nrm_mx.at(n))
            for g in range(2):
                for b in GROUPS[g]:
                    last = nc.tensor.matmul(unit(ps, 8 + b), unit(BD["KB"], b), unit(BD["KB"], b), start=True, stop=True)
                last.then_inc(gram_k.sem, 1)
            pe.wait_ge(qn_ok.sem, qn_ok.at(n))
            if isinstance(n, int) and n == 0:
                pass
            else:
                pe.wait_ge(on_ok.sem, on_ok.at(n - 1))
            for b in range(NB):
                last = nc.tensor.matmul(ps[:, 4 * 512 + b * C:4 * 512 + (b + 1) * C], unit(BD["KB"], b),
                                        qn[:, b * C:(b + 1) * C], start=True, stop=True)
            last.then_inc(gram_p.sem, 1)

        def pe_vtr(pe, n):
            pe.wait_ge(silu.sem, silu.at(n))
            pe.wait_ge(conv.sem, conv.at(n))
            for b in range(NB):
                last = nc.tensor.transpose(unit(ps, b), sv[:, b * P:(b + 1) * P], ident)
            last.then_inc(v_tr.sem, 1)

        def pe_ktr(pe, n):
            pe.wait_ge(v_ok.sem, v_ok.at(n))
            for b in range(NB):
                last = nc.tensor.transpose(unit(ps, b), unit(BD["KB"], b), ident)
            last.then_inc(k_tr.sem, 1)

        def pe_z(pe, n, lv, g):
            if lv == 0:
                pe.wait_ge(nm_ok.sem, nm_ok.at(n, g + 1))
                if g == 0:
                    pe.wait_ge(pt_ok.sem, pt_ok.at(n))
            else:
                pe.wait_ge(y_ok.sem, y_ok.at(n, 2 * (lv - 1) + g + 1))
            for b in GROUPS[g]:
                o = ps[:, (4 + g) * 512 + (b % 4) * P:(4 + g) * 512 + (b % 4 + 1) * P]
                if lv == 0:
                    last = nc.tensor.transpose(o, unit(BD["NM"], b), ident)
                else:
                    last = nc.tensor.matmul(o, unit(BD["X"], b), unit(BD["Y"], b), start=True, stop=True)
            last.then_inc(z_mm.sem, 1)

        def pe_x(pe, n, lv, g):
            pe.wait_ge(z_ok.sem, z_ok.at(n, 2 * lv + g + 1))
            for b in GROUPS[g]:
                o = ps[:, (2 + g) * 512 + (b % 4) * P:(2 + g) * 512 + (b % 4 + 1) * P]
                last = nc.tensor.transpose(o, unit(BD["Z"], b), ident)
            last.then_inc(x_mm.sem, 1)

        def pe_y(pe, n, lv, g):
            pe.wait_ge(x_ok.sem, x_ok.at(n, 2 * (lv - 1) + g + 1))
            for b in GROUPS[g]:
                o = ps[:, (2 + g) * 512 + (b % 4) * P:(2 + g) * 512 + (b % 4 + 1) * P]
                last = nc.tensor.matmul(o, unit(BD["NM"], b), unit(BD["Z"], b), start=True, stop=True)
            last.then_inc(y_mm.sem, 1)

        def pe_invert(pe, n):
            pe_z(pe, n, 0, 0)
            pe_z(pe, n, 0, 1)
            pe_vtr(pe, n)
            for lv in range(1, LEVELS):
                for g in range(2):
                    pe_x(pe, n, lv - 1, g)
                if lv == 1:
                    pe_ktr(pe, n)
                for g in range(2):
                    pe_y(pe, n, lv, g)
                for g in range(2):
                    pe_z(pe, n, lv, g)

        def pe_ks(pe, m):
            pe.wait_ge(kb_ok.sem, kb_ok.at(m))
            if not first(m):
                pe.wait_ge(acc_ok.sem, acc_ok.at(m - 1))
                pe.wait_ge(s_ok.sem, s_ok.at(m - 1))
            for g in range(2):
                for b in GROUPS[g]:
                    last = nc.tensor.matmul(unit(ps, 24 + b), unit(BD["KB"], b), unit(S, b), start=True, stop=True)
                last.then_inc(ks_mm.sem, 1)

        def pe_u(pe, m):
            pe.wait_ge(z_ok.sem, z_ok.at(m))
            for g in range(2):
                pe.wait_ge(r_ok.sem, r_ok.at(m, g + 1))
                for b in GROUPS[g]:
                    last = nc.tensor.matmul(unit(ps, 24 + b), unit(BD["Z"], b), unit(Rr, b), start=True, stop=True)
                last.then_inc(u_mm.sem, 1)

        def pe_o(pe, m):
            pe.wait_ge(qg_ok.sem, qg_ok.at(m))
            pe.wait_ge(pt_ok.sem, pt_ok.at(m))
            for g in range(2):
                pe.wait_ge(u_ok.sem, u_ok.at(m, g + 1))
                for b in GROUPS[g]:
                    nc.tensor.matmul(unit(ps, 16 + b), unit(S, b), unit(BD["QG"], b), start=True, stop=False)
                    last = nc.tensor.matmul(unit(ps, 16 + b), unit(U, b), unit(BD["PT"], b), start=False, stop=True)
                last.then_inc(o_mm.sem, 1)
            pe.wait_ge(kt_ok.sem, kt_ok.at(m))
            for g in range(2):
                for b in GROUPS[g]:
                    last = nc.tensor.matmul(unit(ps, 24 + b), unit(BD["KT"], b), unit(U, b), start=True, stop=True)
                last.then_inc(ds_mm.sem, 1)

        def pe_ms(pe, m):
            for g in range(2):
                pe.wait_ge(s_ok.sem, s_ok.at(m, g + 1))
                pe.wait_ge(o_sq.sem, o_sq.at(m, g + 1))
                nc.tensor.matmul(bank(6 + g), kc(K_ONE), osq[:, g * 512:(g + 1) * 512], start=True, stop=True).then_inc(ms_mm.sem, 1)

        def pe_wo(pe, m):
            pe.wait_ge(on_ok.sem, on_ok.at(m))
            pe.wait_ge(wo_in.sem, wo_in.at(m))
            on4 = on[:].rearrange("p (b h t) -> p b h t", b=NB, h=2)
            for h in range(2):
                last = nc.tensor.matmul(bank(6), wo_s[:, h * D:(h + 1) * D], on4[:, :, h, :], start=(h == 0), stop=(h == 1))
            last.then_inc(wo_mm.sem, 1)

        def pe_body(pe, m, n):
            if m is not None:
                pe_ks(pe, m)
            if n is not None:
                pe_proj(pe, n, 0)
                pe_decay(pe, n)
            if m is not None:
                pe_u(pe, m)
            if n is not None:
                pe_proj(pe, n, 1)
                pe_decay_g(pe, n)
            if m is not None:
                pe_o(pe, m)
            if n is not None:
                pe_proj(pe, n, 2)
                pe_norm(pe, n, 0)
            if m is not None:
                pe_ms(pe, m)
            if n is not None:
                pe_norm(pe, n, 1)
                pe_proj(pe, n, 3)
            if m is not None:
                pe_wo(pe, m)
            if n is not None:
                pe_gram(pe, n)
                pe_invert(pe, n)

        def act_tap0(act, n, j):
            act.wait_ge(proj.sem, proj.at(n, j + 1))
            if not first(n):
                act.wait_ge(silu.sem, silu.at(n - 1, j + 1))
            nc.scalar.activation(cv4[:, j], pj[:, :, 0:C], ACT.Copy, scale=w_s[:, 512 + 4 * j:513 + 4 * j]).then_inc(tap0.sem, 1)

        def act_exp(act, n, i):
            act.wait_ge(dec_mm.sem, dec_mm.at(n, i + 1))
            if not first(n):
                if i < 2:
                    act.wait_ge(pt_ok.sem, pt_ok.at(n - 1))
                    act.wait_ge(nm_ok.sem, nm_ok.at(n - 1))
                else:
                    act.wait_ge(qg_ok.sem, qg_ok.at(n - 1))
            nc.scalar.activation(ex[:, i * 512:(i + 1) * 512], bank((2, 3, 2)[i]), ACT.Exp).then_inc(dec_ex.sem, 1)

        def act_silu(act, n, j):
            act.wait_ge(conv.sem, conv.at(n, 3 * j + 3))
            if j < 2:
                if not first(n):
                    act.wait_ge(kb_ok.sem, kb_ok.at(n - 1))
                    act.wait_ge(qn_ok.sem, qn_ok.at(n - 1))
                    act.wait_ge(sqr.sem, sqr.at(n - 1))
                o = v3(sl, j)
            else:
                if not first(n):
                    act.wait_ge(v_tr.sem, v_tr.at(n - 1))
                o = sv4[:, :, j - 2, :]
            nc.scalar.activation(o, cv4[:, j], ACT.Silu).then_inc(silu.sem, 1)

        def act_norm(act, n, i):
            act.wait_ge(nrm_mx.sem, nrm_mx.at(n, i + 1))
            r = rn[:, i * 512:(i + 1) * 512]
            nc.scalar.activation(r, r, ACT.Ln).then_inc(nrm_ln.sem, 1)
            act.wait_ge(nrm_ln.sem, nrm_ln.at(n, i + 1))
            nc.scalar.activation(r, r, ACT.Exp, scale=-0.5).then_inc(nrm_rn.sem, 1)

        def act_copy_half(o, s):
            return nc.scalar.activation(o, s, ACT.Copy)

        def act_x(act, n, lv, g):
            act.wait_ge(x_mm.sem, x_mm.at(n, 2 * lv + g + 1))
            act_copy_half(BD["X"][:, g * 512:(g + 1) * 512], bank(2 + g)).then_inc(x_ok.sem, 1)

        def act_y(act, n, lv, g):
            act.wait_ge(y_mm.sem, y_mm.at(n, 2 * (lv - 1) + g + 1))
            act_copy_half(BD["Y"][:, g * 512:(g + 1) * 512], bank(2 + g)).then_inc(y_ok.sem, 1)

        def act_invert(act, n):
            act.wait_ge(v_tr.sem, v_tr.at(n))
            if not first(n):
                act.wait_ge(r_ok.sem, r_ok.at(n - 1))
            nc.scalar.activation(Vt[:], bank(0, 2), ACT.Copy).then_inc(v_ok.sem, 1)
            for lv in range(1, LEVELS):
                for g in range(2):
                    act_x(act, n, lv - 1, g)
                for g in range(2):
                    act_y(act, n, lv, g)

        def act_u(act, m):
            for g in range(2):
                act.wait_ge(u_mm.sem, u_mm.at(m, g + 1))
                if not first(m):
                    act.wait_ge(ds_mm.sem, ds_mm.at(m - 1))
                act_copy_half(U[:, g * 512:(g + 1) * 512], bank(6 + g)).then_inc(u_ok.sem, 1)

        def act_osq(act, m):
            for g in range(2):
                act.wait_ge(o_mm.sem, o_mm.at(m, g + 1))
                if not first(m):
                    act.wait_ge(ms_mm.sem, ms_mm.at(m - 1, g + 1))
                nc.scalar.activation(osq[:, g * 512:(g + 1) * 512], bank(4 + g), ACT.Square).then_inc(o_sq.sem, 1)

        def act_orn(act, m):
            for g in range(2):
                r = orn[:, g * 512:(g + 1) * 512]
                act.wait_ge(ms_mm.sem, ms_mm.at(m, g + 1))
                if not first(m):
                    act.wait_ge(on_ok.sem, on_ok.at(m - 1, g + 1))
                nc.scalar.activation(r, bank(6 + g), ACT.Ln, bias=eps[:, 1:2]).then_inc(ms_ln.sem, 1)
                act.wait_ge(ms_ln.sem, ms_ln.at(m, g + 1))
                nc.scalar.activation(r, r, ACT.Exp, scale=-0.5).then_inc(ms_rn.sem, 1)

        def act_body(act, m, n):
            if n is not None:
                act_tap0(act, n, 0)
                act_exp(act, n, 0)
                act_exp(act, n, 1)
            if m is not None:
                act_u(act, m)
            if n is not None:
                act_tap0(act, n, 1)
                act_exp(act, n, 2)
            if m is not None:
                act_osq(act, m)
            if n is not None:
                act_tap0(act, n, 2)
                act.preload_act_table_set("silu_and_others")
                act_silu(act, n, 0)
                act_silu(act, n, 1)
                act_tap0(act, n, 3)
                act_silu(act, n, 2)
                act_silu(act, n, 3)
                act.preload_act_table_set("natural_log_exp_and_others")
            if m is not None:
                act_orn(act, m)
            if n is not None:
                act_norm(act, n, 0)
                act_norm(act, n, 1)
                act_invert(act, n)

        def dve_conv(dve, n, j):
            for k in range(1, TAPS):
                if k == 1:
                    dve.wait_ge(tap0.sem, tap0.at(n, j + 1))
                else:
                    dve.wait_ge(conv.sem, conv.at(n, 3 * j + k - 1))
                nc.vector.scalar_tensor_tensor(cv4[:, j], pj[:, :, k:k + C], w_s[:, 512 + 4 * j + k:513 + 4 * j + k], cv4[:, j],
                                               ALU.mult, ALU.add).then_inc(conv.sem, 1)

        def dve_norm_max(dve, n, i):
            dve.wait_ge(nrm_mm.sem, nrm_mm.at(n, i + 1))
            if not first(n):
                dve.wait_ge(kb_ok.sem, kb_ok.at(n - 1))
                dve.wait_ge(qn_ok.sem, qn_ok.at(n - 1))
            nc.vector.tensor_scalar(rn[:, i * 512:(i + 1) * 512], bank(3 - i), EPS_L2 * EPS_L2, None, ALU.max).then_inc(nrm_mx.sem, 1)

        def dve_keys(dve, n):
            dve.wait_ge(nrm_rn.sem, nrm_rn.at(n, 1))
            if not first(n):
                dve.wait_ge(ks_mm.sem, ks_mm.at(n - 1))
                dve.wait_ge(k_tr.sem, k_tr.at(n - 1))
            for a, z in HALF:
                last = nc.vector.tensor_tensor(bd("KB")[a:z, :, a:z], v3(sl, 0)[a:z], v3(rn, 0)[a:z], ALU.mult)
            last.then_inc(kb_ok.sem, 1)
            dve.wait_ge(nrm_rn.sem, nrm_rn.at(n, 2))
            if not first(n):
                dve.wait_ge(gram_p.sem, gram_p.at(n - 1))
                dve.wait_ge(qg_ok.sem, qg_ok.at(n - 1))
            nc.vector.tensor_tensor(qn[:], sl[:, 512:1024], rn[:, 512:1024], ALU.mult).then_inc(qn_ok.sem, 1)

        def dve_mats(dve, n):
            if not first(n):
                dve.wait_ge(y_mm.sem, y_mm.at(n - 1))
                dve.wait_ge(o_mm.sem, o_mm.at(n - 1))
            dve.wait_ge(dmul.sem, dmul.at(n, 2))
            gk = bank(2, 2).rearrange("p (b c) -> p b c", b=NB)
            for g in range(2):
                dve.wait_ge(gram_k.sem, gram_k.at(n, g + 1))
                for a, z in HALF:
                    last = nc.vector.tensor_tensor(bd("NM")[a:z, 4 * g:4 * g + 4, a:z], gk[a:z, 4 * g:4 * g + 4, a:z],
                                                   v3(ex, 0)[a:z, 4 * g:4 * g + 4, :], ALU.mult)
                last.then_inc(nm_ok.sem, 1)
            dve.wait_ge(dmul.sem, dmul.at(n, 3))
            dve.wait_ge(gram_p.sem, gram_p.at(n))
            gp = bank(4).rearrange("p (b t) -> p b t", b=NB)
            for a, z in HALF:
                last = nc.vector.tensor_tensor(bd("PT")[a:z, :, a:z], gp[a:z], v3(ex, 1)[a:z], ALU.mult)
            last.then_inc(pt_ok.sem, 1)

        def dve_z(dve, n, lv, g):
            dve.wait_ge(z_mm.sem, z_mm.at(n, 2 * lv + g + 1))
            if lv == 0 and g == 0:
                dve.wait_ge(z_one.sem, z_one.at(n))
            dve.sem_inc(z_go.sem, 1)
            nc.vector.copy_predicated(bd("Z")[:, 4 * g:4 * g + 4, :], over(LMASK[lv], 4, P),
                                      bank(4 + g).rearrange("p (b c) -> p b c", b=4)).then_inc(z_ok.sem, 1)

        def dve_invert(dve, n):
            for lv in range(LEVELS):
                for g in range(2):
                    dve_z(dve, n, lv, g)
                if lv == 1:
                    dve.wait_ge(k_tr.sem, k_tr.at(n))
                    dve.wait_ge(st_ok.sem, st_ok.at(n))
                    if not first(n):
                        dve.wait_ge(ds_mm.sem, ds_mm.at(n - 1))
                    for g in range(2):
                        last = nc.vector.tensor_tensor(bd("KT")[:, 4 * g:4 * g + 4, :], bank(g).rearrange("p (b c) -> p b c", b=4),
                                                       bcast(stP[:, 16:24], P)[:, 4 * g:4 * g + 4, :], ALU.mult)
                    last.then_inc(kt_ok.sem, 1)

        def dve_r(dve, m):
            dve.wait_ge(stR_ok.sem, stR_ok.at(m))
            dve.wait_ge(v_ok.sem, v_ok.at(m))
            for g in range(2):
                dve.wait_ge(ks_mm.sem, ks_mm.at(m, g + 1))
                if not first(m):
                    dve.wait_ge(u_mm.sem, u_mm.at(m - 1))
                for b in GROUPS[g]:
                    last = nc.vector.scalar_tensor_tensor(unit(Rr, b), unit(ps, 24 + b), stR[:, b:b + 1], unit(Vt, b), ALU.mult, ALU.add)
                last.then_inc(r_ok.sem, 1)

        def dve_s(dve, m):
            dve.wait_ge(o_mm.sem, o_mm.at(m))
            for g in range(2):
                dve.wait_ge(ds_mm.sem, ds_mm.at(m, g + 1))
                for b in GROUPS[g]:
                    last = nc.vector.scalar_tensor_tensor(unit(S, b), unit(S, b), stR[:, 8 + b:9 + b], unit(ps, 24 + b), ALU.mult, ALU.add)
                last.then_inc(s_ok.sem, 1)

        def dve_on(dve, m):
            if not first(m):
                dve.wait_ge(wo_mm.sem, wo_mm.at(m - 1))
            for g in range(2):
                dve.wait_ge(ms_rn.sem, ms_rn.at(m, g + 1))
                nc.vector.tensor_tensor(on[:, g * 512:(g + 1) * 512], bank(4 + g), orn[:, g * 512:(g + 1) * 512], ALU.mult).then_inc(on_ok.sem, 1)

        def dve_acc(dve, m):
            dve.wait_ge(wo_mm.sem, wo_mm.at(m))
            if not first(m):
                dve.wait_ge(acc_ok.sem, acc_ok.at(m - 1))
            dst = accT3[:, :, bass.ds((m % NC) * C, C)]
            nc.vector.tensor_tensor(dst, bank(6).rearrange("p (b t) -> p b t", b=NB), dst, ALU.add).then_inc(acc_ok.sem, 1)

        def dve_body(dve, m, n):
            if m is not None:
                if not first(m):
                    dve.wait_ge(s_ok.sem, s_ok.at(m - 1))
                nc.vector.tensor_copy(stR[:].rearrange("p (o k) -> p o k", o=1), tabR3[:, bass.ds(m, 1), :]).then_inc(stR_ok.sem, 1)
            if n is not None:
                dve_conv(dve, n, 0)
            if m is not None:
                dve_r(dve, m)
            if n is not None:
                dve_conv(dve, n, 1)
                dve_conv(dve, n, 2)
            if m is not None:
                dve_s(dve, m)
            if n is not None:
                dve_norm_max(dve, n, 0)
                dve_norm_max(dve, n, 1)
                dve_conv(dve, n, 3)
            if m is not None:
                dve_on(dve, m)
            if n is not None:
                dve_keys(dve, n)
            if m is not None:
                dve_acc(dve, m)
            if n is not None:
                dve_mats(dve, n)
                dve_invert(dve, n)

        def pool_body(pool, m, n):
            if n is None:
                return
            pool.wait_ge(cexp.sem, 2)
            if not first(n):
                pool.wait_ge(kt_ok.sem, kt_ok.at(n - 1))
                pool.wait_ge(dmul.sem, dmul.at(n - 1))
                pool.wait_ge(qg_ok.sem, qg_ok.at(n - 1))
            nc.gpsimd.tensor_copy(stP[:].rearrange("p (o k) -> p o k", o=1), tabP3[:, bass.ds(n, 1), :]).then_inc(st_ok.sem, 1)
            pool.wait_ge(st_ok.sem, st_ok.at(n))
            if not first(n):
                pool.wait_ge(dec_mm.sem, dec_mm.at(n - 1))
            for i, o in enumerate((K_MGT, K_MLE)):
                nc.gpsimd.tensor_tensor(v3(Lm, i), over(kc(o, C), NB, C), bcast(stP[:, 0:8], C), ALU.mult).then_inc(lm_ok.sem, 1)
            pool.wait_ge(dec_ex.sem, dec_ex.at(n, 1))
            nc.gpsimd.tensor_tensor(v3(ex, 0), v3(ex, 0), over(kc(K_NEG, C), NB, C), ALU.mult).then_inc(dmul.sem, 1)
            pool.wait_ge(dmul.sem, dmul.at(n, 1))
            nc.gpsimd.tensor_tensor(v3(ex, 0), v3(ex, 0), bcast(stP[:, 8:16], C), ALU.mult).then_inc(dmul.sem, 1)
            pool.wait_ge(dec_ex.sem, dec_ex.at(n, 2))
            nc.gpsimd.tensor_tensor(v3(ex, 1), v3(ex, 1), over(kc(K_MLE, C), NB, C), ALU.mult).then_inc(dmul.sem, 1)
            for i in range(2):
                pool.wait_ge(silu.sem, silu.at(n, i + 1))
                if not first(n):
                    pool.wait_ge(nrm_mm.sem, nrm_mm.at(n - 1, i + 1))
                s = sl[:, i * 512:(i + 1) * 512]
                nc.gpsimd.tensor_tensor(sq[:, i * 512:(i + 1) * 512], s, s, ALU.mult).then_inc(sqr.sem, 1)
            pool.wait_ge(c_in.sem, 64)
            if m is not None:
                pool.wait_ge(u_mm.sem, u_mm.at(m))
            nc.gpsimd.tensor_copy(bd("Z"), over(ident, NB, P)).then_inc(z_one.sem, 1)
            pool.wait_ge(qn_ok.sem, qn_ok.at(n))
            pool.wait_ge(dec_ex.sem, dec_ex.at(n, 3))
            if m is not None:
                pool.wait_ge(o_mm.sem, o_mm.at(m))
            pool.wait_ge(z_one.sem, z_one.at(n))
            for i, (a, z) in enumerate(HALF):
                if i:
                    pool.wait_ge(qg_ok.sem, qg_ok.at(n, i))
                nc.gpsimd.tensor_tensor(bd("QG")[a:z, :, a:z], qn[a:z].rearrange("p (b t) -> p b t", b=NB), v3(ex, 2)[a:z],
                                        ALU.mult).then_inc(qg_ok.sem, 1)

        def sp_body(sp, m, n):
            if m is not None:
                if not first(m):
                    sp.wait_ge(wo_mm.sem, wo_mm.at(m - 1))
                sp.dma_start(wo_s[:].rearrange("p (o k) -> p o k", o=1), wo[:, bass.ds(m // NC, 1), :]).then_inc(wo_in.sem, 16)
            if n is not None:
                if not first(n):
                    sp.wait_ge(conv.sem, conv.at(n - 1))
                    sp.wait_ge(proj.sem, proj.at(n - 1))
                sp.dma_start(w_s[:].rearrange("p (o k) -> p o k", o=1), wtab[:, bass.ds(n // NC, 1), :]).then_inc(w_in.sem, 16)

        def program(eng, body):
            body(eng, None, 0)
            body(eng, 0, 1)
            with eng.Fori(1, STEPS - 1) as i:
                body(eng, i, i + 1)
            body(eng, STEPS - 1, None)

        with nc.Block() as block:
            @block.sync
            def _(sp):
                program(sp, sp_body)

            @block.gpsimd
            def _(pool):
                program(pool, pool_body)

            @block.scalar
            def _(act):
                act.preload_act_table_set("natural_log_exp_and_others")
                program(act, act_body)

            @block.vector
            def _(dve):
                program(dve, dve_body)

            @block.tensor
            def _(pe):
                program(pe, pe_body)

        f_w = sig("f_w")
        f_x = sig("f_x")
        f_at = sig("f_at")
        f_tr = sig("f_tr")
        f_ch = sig("f_ch")
        f_st = sig("f_st", 3)
        f_sd = sig("f_sd", 3)
        f_x1 = sig("f_x1")
        f_n1 = sig("f_n1")
        f_t2 = sig("f_t2")
        f_ev = sig("f_ev")
        f_mx = sig("f_mx")
        f_k = sig("f_k", 2)
        f_rl = sig("f_rl", 2)
        f_sqk = sig("f_sqk")
        f_r = sig("f_r")
        f_sg = sig("f_sg")
        f_v = sig("f_v")
        f_y = sig("f_y")
        f_out = sig("f_out")
        a_s, x_s, x1, n1, hT, dT, xr, xk, ka, rg, yo = (BD["KB"], BD["QG"], BD["PT"], BD["NM"], BD["Z"], BD["X"], BD["Y"], BD["KT"], Vt, Rr, U)
        rl = S
        zc = small[:, 128:129]
        hx = sb("hx", 1 + T)
        wf_s = sb("wf_s", 3 * P)
        out_tok = out.rearrange("b (j p) d -> b p j d", p=P)
        t3 = lambda t: t[:].rearrange("p (j d) -> p j d", j=NT)

        with nc.Block() as block:
            @block.sync
            def _(sp):
                sp.dma_start(wf_s[:], wf).then_inc(f_w.sem, 16)
                for b in range(NB):
                    if b:
                        sp.wait_ge(f_x1.sem, b)
                    sp.dma_start(t3(x_s), x_tok[b]).then_inc(f_x.sem, 16)
                    sp.wait_ge(f_y.sem, b + 1)
                    sp.dma_start(out_tok[b], t3(yo)).then_inc(f_out.sem, 16)
                sp.wait_ge(f_out.sem, 16 * NB)

            @block.gpsimd
            def _(pool):
                nc.gpsimd.memset(hx[:, 0:1], 0.0).then_inc(zeroed.sem, 1)

            @block.vector
            def _(dve):
                chain = [0]

                def then(ins):
                    chain[0] += 1
                    ins.then_inc(f_ch.sem, 1)
                    dve.wait_ge(f_ch.sem, chain[0])

                def norm(src, dst, b, k):
                    st = small[:, 0:6 * NT].rearrange("p (j k) -> p j k", j=NT)
                    ag = small[:, 64:64 + 2 * NT].rearrange("p (j k) -> p j k", j=NT)
                    for j in range(NT):
                        last = nc.vector.bn_stats(st[:, j, :], src[:, j, :])
                    then(last)
                    for j in range(NT):
                        last = nc.vector.bn_aggr(ag[:, j, :], st[:, j, :])
                    last.then_inc(f_st.sem, 1)
                    dve.wait_ge(f_sd.sem, 3 * b + k + 1)
                    then(nc.vector.reciprocal(small[:, 96:96 + NT], small[:, 88:88 + NT]))
                    for j in range(NT):
                        last = nc.vector.tensor_scalar(dst[:, j, :], src[:, j, :], ag[:, j, 0:1], small[:, 96 + j:97 + j],
                                                       ALU.subtract, ALU.mult)
                    then(last)

                for b in range(NB):
                    dve.wait_ge(f_tr.sem, b + 1)
                    norm(bank(0, 2).rearrange("p (j d) -> p j d", j=NT), t3(x1), b, 0)
                    dve.wait_ge(f_x.sem, 16 * (b + 1))
                    then(nc.vector.tensor_tensor(x1[:], x1[:], x_s[:], ALU.add))
                    dve.sem_inc(f_x1.sem, 1)
                    if b:
                        dve.wait_ge(f_t2.sem, b)
                    norm(t3(x1), t3(n1), b, 1)
                    dve.sem_inc(f_n1.sem, 1)
                    dve.wait_ge(f_ev.sem, b + 1)
                    if b:
                        dve.wait_ge(f_r.sem, b)
                    then(nc.vector.tensor_tensor(dT[:], hx[:, 1:1 + T], hx[:, 0:T], ALU.subtract))
                    nc.vector.scalar_tensor_tensor(xr[:], dT[:], muc[:, 0:1], hx[:, 0:T], ALU.mult, ALU.add)
                    then(nc.vector.scalar_tensor_tensor(xk[:], dT[:], muc[:, 1:2], hx[:, 0:T], ALU.mult, ALU.add))
                    dve.sem_inc(f_mx.sem, 1)
                    dve.wait_ge(f_rl.sem, f_rl.at(b))
                    if b:
                        dve.wait_ge(f_v.sem, b)
                    then(nc.vector.tensor_tensor(ka[:], rl[:], rl[:], ALU.mult))
                    dve.sem_inc(f_sqk.sem, 1)
                    dve.wait_ge(f_v.sem, b + 1)
                    dve.wait_ge(f_sg.sem, b + 1)
                    if b:
                        dve.wait_ge(f_out.sem, 16 * b)
                    then(nc.vector.tensor_tensor(rg[:], bank(4, 2), rg[:], ALU.mult))
                    norm(t3(rg), t3(yo), b, 2)
                    then(nc.vector.tensor_tensor(yo[:], yo[:], x1[:], ALU.add))
                    dve.sem_inc(f_y.sem, 1)

            @block.scalar
            def _(act):
                def root(b, k):
                    act.wait_ge(f_st.sem, 3 * b + k + 1)
                    ag = small[:, 64:64 + 2 * NT].rearrange("p (j k) -> p j k", j=NT)
                    nc.scalar.activation(small[:, 88:88 + NT], ag[:, :, 1], ACT.Sqrt, bias=eps[:, 0:1]).then_inc(f_sd.sem, 1)

                for b in range(NB):
                    if b:
                        act.wait_ge(f_tr.sem, b)
                    nc.scalar.activation(a_s[:], accT3[:, b, :], ACT.Copy).then_inc(f_at.sem, 1)
                    root(b, 0)
                    root(b, 1)
                    act.wait_ge(f_t2.sem, b + 1)
                    if b:
                        act.wait_ge(f_mx.sem, b)
                    nc.scalar.activation(hx[:, 1:1 + T], bank(2, 2), ACT.Copy).then_inc(f_ev.sem, 1)
                    for k in range(2):
                        act.wait_ge(f_k.sem, 2 * b + k + 1)
                        if b:
                            act.wait_ge(f_sqk.sem, b)
                        nc.scalar.activation(rl[:, k * 512:(k + 1) * 512], bank(k), ACT.Relu).then_inc(f_rl.sem, 1)
                    act.wait_ge(f_r.sem, b + 1)
                    if b:
                        act.wait_ge(f_y.sem, b)
                    nc.scalar.activation(rg[:], bank(2, 2), ACT.Sigmoid).then_inc(f_sg.sem, 1)
                    root(b, 2)

            @block.tensor
            def _(pe):
                pe.wait_ge(zeroed.sem, 5)
                pe.wait_ge(f_w.sem, 16)
                for b in range(NB):
                    pe.wait_ge(f_at.sem, b + 1)
                    if b:
                        pe.wait_ge(f_rl.sem, f_rl.at(b - 1))
                    for j in range(NT):
                        last = nc.tensor.transpose(unit(ps, j), unit(a_s, j), ident)
                    last.then_inc(f_tr.sem, 1)
                    pe.wait_ge(f_n1.sem, b + 1)
                    if b:
                        pe.wait_ge(f_sg.sem, b)
                    for j in range(NT):
                        last = nc.tensor.transpose(unit(ps, 8 + j), unit(n1, j), ident)
                    last.then_inc(f_t2.sem, 1)
                    pe.wait_ge(f_mx.sem, b + 1)
                    for k in range(2):
                        nc.tensor.matmul(bank(k), wf_s[:, P:2 * P], xk[:, k * 512:(k + 1) * 512], start=True, stop=True).then_inc(f_k.sem, 1)
                    for j in range(NT):
                        last = nc.tensor.matmul(unit(ps, 8 + j), unit(xr, j), wf_s[:, 0:P], start=True, stop=True)
                    last.then_inc(f_r.sem, 1)
                    pe.wait_ge(f_sqk.sem, b + 1)
                    if b:
                        pe.wait_ge(f_y.sem, b)
                    for j in range(NT):
                        last = nc.tensor.matmul(unit(ps, 16 + j), unit(ka, j), wf_s[:, 2 * P:3 * P], start=True, stop=True)
                    last.then_inc(f_v.sem, 1)


def kernel(L0_attn_x, L0_attn_Wq, L0_attn_Wk, L0_attn_Wv, L0_attn_Wb, L0_attn_Wa, L0_attn_A_log, L0_attn_dt_bias,
           L0_attn_Wo, L0_attn_conv_q, L0_attn_conv_k, L0_attn_conv_v, L0_ffn_W_r, L0_ffn_W_k, L0_ffn_W_v,
           L0_ffn_mu_r, L0_ffn_mu_k):
    import concourse.bacc as bacc
    from concourse.bass_utils import run_bass_kernel_spmd

    f = lambda a: np.asarray(a)
    wk = f(L0_attn_Wk).reshape(HP, P, D)
    wq = f(L0_attn_Wq).reshape(HP, P, D)
    wv = f(L0_attn_Wv).reshape(HP, 2, P, D)
    w = np.stack([wk, wq, wv[:, 0], wv[:, 1]], 1)
    w = w.transpose(3, 0, 1, 2).reshape(D, HP, 4 * P)
    ck = f(L0_attn_conv_k).reshape(HP, P, TAPS)
    cq = f(L0_attn_conv_q).reshape(HP, P, TAPS)
    cvw = f(L0_attn_conv_v).reshape(HP, 2, P, TAPS)
    taps = np.stack([ck, cq, cvw[:, 0], cvw[:, 1]], 1).transpose(2, 0, 1, 3).reshape(P, HP, 4 * TAPS)
    wtab = np.concatenate([w, taps], 2)
    wo = f(L0_attn_Wo).reshape(D, HP, 2, DV).transpose(3, 1, 2, 0).reshape(DV, HP, 2 * D)
    wa = f(L0_attn_Wa).reshape(HP, 2, D).transpose(2, 1, 0)
    wb = f(L0_attn_Wb).reshape(HP, 2, D).transpose(2, 1, 0)
    wab = np.concatenate([wa, wb], 2).reshape(D, 32)
    col = lambda a: np.repeat(f(a).reshape(HP, 2).T, C, axis=0)
    hcol = np.concatenate([col(L0_attn_dt_bias), col(L0_attn_A_log)], 1)
    wf = np.concatenate([f(L0_ffn_W_r).T, f(L0_ffn_W_k).T, f(L0_ffn_W_v).T], 1)
    mu = np.stack([f(L0_ffn_mu_r), f(L0_ffn_mu_k)], 1)
    arrays = {"x": f(L0_attn_x), "wtab": wtab, "wo": wo, "wab": wab, "hcol": hcol, "cst": constants(), "wf": wf, "mu": mu}
    arrays = {k: np.ascontiguousarray(v) for k, v in arrays.items()}
    nc = bacc.Bacc("TRN2", target_bir_lowering=False, num_devices=1)
    args = [nc.dram_tensor(k, v.shape, mybir.dt.from_np(v.dtype), kind="ExternalInput").ap() for k, v in arrays.items()]
    out = nc.dram_tensor("out", (NB, T, D), F32, kind="ExternalOutput").ap()
    build(nc, *args, out)
    r = run_bass_kernel_spmd(nc, [arrays], core_ids=[0])
    return r.results[0]["out"]
```

```python
import numpy as np
import concourse.bass as bass
from concourse import mybir
from contextlib import ExitStack

F32 = mybir.dt.float32
U32 = mybir.dt.uint32
ALU = mybir.AluOpType
ACT = mybir.ActivationFunctionType

P = 128
NB = 8
T = 1024
D = 128
H = 16
HP = H // 2
DK = 64
DV = 128
C = 64
NC = T // C
STEPS = HP * NC
TAPS = 4
HALO = TAPS - 1
CW = C + HALO
NT = T // P
LEVELS = (4, 5)
SUBS = 17
SK = 16 * C + 16
SB = NB * SK
C_IN = 80
HALF = ((0, 64), (64, 128))
RESET = -1.0e4
EPS_LN = 1e-5
EPS_L2 = 1e-6
EPS_RMS = 1e-6

K_ID, K_LE, K_GT, K_BD, K_ONE, K_MGT, K_MLE, K_LV = 0, 128, 256, 384, 512, 640, 704, 768
K_XI = K_LV + len(LEVELS) * P
K_N = K_XI + 272


def constants():
    c = np.zeros((P, K_N), np.float32)
    i = np.arange(P)
    same = (i[:, None] // C) == (i[None, :] // C)
    r, t = (i % C)[:, None], (i % C)[None, :]
    c[:, K_ID:K_ID + P] = np.eye(P)
    c[:, K_LE:K_LE + P] = same & (r <= t)
    c[:, K_GT:K_GT + P] = same & (r > t)
    c[:, K_BD:K_BD + P] = same
    c[:, K_ONE:K_ONE + P] = 1.0 / DV
    j = np.arange(C)[None, :]
    c[:, K_MGT:K_MGT + C] = r > j
    c[:, K_MLE:K_MLE + C] = r <= j
    for k, lv in enumerate(LEVELS):
        n = 1 << lv
        c[:, K_LV + k * P:K_LV + (k + 1) * P] = same & (r // n % 2 == 0) & (t // n == r // n + 1)
    c[:, K_XI:K_XI + 256:17] = 1.0
    return c


class Signal:

    def __init__(self, sem, per):
        self.sem, self.per = sem, per

    def at(self, step, k=None):
        return step * self.per + (self.per if k is None else k)


AX = mybir.AxisListType.X


def build(nc, x, wtab, wo, wab, hcol, cst, wf, mu, out):
    with ExitStack() as ctx:
        def sb(name, cols, dt=F32):
            return ctx.enter_context(nc.sbuf_tensor(name, [P, cols], dt))

        def sig(name, per=1):
            return Signal(ctx.enter_context(nc.semaphore(name)), per)

        k_all = sb("k_all", K_N)
        xnT = sb("xnT", NB * (HALO + T))
        accT = sb("accT", NB * T)
        tabP = sb("tabP", STEPS * 24)
        tabR = sb("tabR", STEPS * 16)
        xnT3 = xnT[:].rearrange("p (b t) -> p b t", b=NB)
        accT3 = accT[:].rearrange("p (b t) -> p b t", b=NB)
        w_kq = sb("w_kq", 2 * P + 2 * TAPS)
        w_v = sb("w_v", 2 * P + 2 * TAPS)
        wo_s = sb("wo_s", 2 * D)
        stP = sb("stP", 24)
        stR = sb("stR", 16)
        Lm = sb("Lm", 2 * 512)
        ex = sb("ex", 3 * 512)
        cv = sb("cv", 4 * 512)
        sl = sb("sl", 2 * 512)
        sv = sb("sv", 1024)
        sq = sb("sq", 2 * 512)
        qn = sb("qn", 512)
        BD = {n: sb(n, NB * P) for n in ("KB", "QG", "PT", "NM", "Z", "X", "Y", "KT")}
        Vt = sb("Vt", NB * P)
        Rr = sb("Rr", NB * P)
        U = sb("U", NB * P)
        S = sb("S", NB * P)
        oo = sb("oo", 1024)
        Nd = sb("Nd", 512)
        NS = sb("NS", 272)
        XT = sb("XT", 272)
        tmpS = sb("tmpS", 512)
        tmpW = sb("tmpW", 64)
        scrN = nc.dram_tensor("scrN", (NB * SB,), F32, kind="Internal").ap()
        scrZ = nc.dram_tensor("scrZ", (NB * SB,), F32, kind="Internal").ap()
        eps = sb("eps", 4)
        small = sb("small", 256)
        hc = sb("hc", 16)
        muc = sb("muc", 2)

        def bd(n):
            return BD[n][:].rearrange("p (b c) -> p b c", b=NB)

        ps = ctx.enter_context(nc.psum_tensor("ps", [P, 8 * 512], F32))

        def bank(i, n=1):
            return ps[:, i * 512:(i + n) * 512]

        def kc(o, n=P):
            return k_all[:, o:o + n]

        ident = kc(K_ID)

        def bcast(ap, n):
            return ap.rearrange("p (b o) -> p b o", o=1).to_broadcast([P, NB, n])

        def over(ap, b, n):
            return ap.rearrange("p (o n) -> p o n", o=1).to_broadcast([P, b, n])

        c_in = sig("c_in")
        x_in = [sig("x_in0"), sig("x_in1")]
        x_free = sig("x_free")
        zeroed = sig("zeroed")
        scr_z = sig("scr_z")
        stats = sig("stats")
        rstd_s = sig("rstd_s")
        rstd_v = sig("rstd_v")
        xn_ok = sig("xn_ok")
        xn_tr = sig("xn_tr")
        xn_ev = sig("xn_ev")
        dchain = sig("dchain")
        lin = sig("lin")
        zz = sig("zz")
        a_step = sig("a_step")
        v_step = sig("v_step")
        cum = sig("cum")
        cexp = sig("cexp")

        xt = [KBuf for KBuf in (BD["KB"], BD["QG"])]
        xn = [BD["PT"], BD["NM"]]
        wab_s = cv[:, 0:32]
        la = Vt
        be = Rr
        tmp = [U, S]
        x_tok = x.rearrange("b (j p) d -> b p j d", p=P)
        pairs = [(b // 2, b % 2) for b in range(NB)]

        with nc.Block() as block:
            @block.sync
            def _(sp):
                sp.dma_start(k_all[:], cst).then_inc(c_in.sem, 16)
                sp.dma_start(wab_s, wab).then_inc(c_in.sem, 16)
                sp.dma_start(hc[:], hcol).then_inc(c_in.sem, 16)
                sp.dma_start(muc[:], mu).then_inc(c_in.sem, 16)
                sp.dma_start(XT[:], cst[:, K_XI:K_XI + 272]).then_inc(c_in.sem, 16)
                for b in range(NB):
                    if b >= 2:
                        sp.wait_ge(x_free.sem, b - 1)
                    sp.dma_start(xt[b % 2][:].rearrange("p (j d) -> p j d", j=NT), x_tok[b]).then_inc(x_in[b % 2].sem, 16)

            @block.gpsimd
            def _(pool):
                nc.gpsimd.memset(eps[:, 0:1], EPS_LN).then_inc(zeroed.sem, 1)
                nc.gpsimd.memset(eps[:, 1:2], EPS_RMS).then_inc(zeroed.sem, 1)
                nc.gpsimd.memset(eps[:, 2:3], EPS_L2 * EPS_L2).then_inc(zeroed.sem, 1)
                nc.gpsimd.memset(eps[:, 3:4], -EPS_L2 * EPS_L2).then_inc(zeroed.sem, 1)
                nc.gpsimd.memset(xnT3[:, :, 0:HALO], 0.0).then_inc(zeroed.sem, 1)
                nc.gpsimd.memset(accT[:], 0.0).then_inc(zeroed.sem, 1)
                pool.wait_ge(zeroed.sem, 6)
                pool.dma_start(scrZ.rearrange("(p k) -> p k", p=P), accT[:, 0:NB * SB // P]).then_inc(scr_z.sem, 16)
                pool.wait_ge(scr_z.sem, 16)

            @block.vector
            def _(dve):
                chain = [0]

                def then(ins):
                    chain[0] += 1
                    ins.then_inc(dchain.sem, 1)
                    dve.wait_ge(dchain.sem, chain[0])

                for b in range(NB):
                    src = xt[b % 2][:].rearrange("p (j d) -> p j d", j=NT)
                    dst = xn[b % 2][:].rearrange("p (j d) -> p j d", j=NT)
                    dve.wait_ge(x_in[b % 2].sem, 16 * (b // 2 + 1))
                    st = small[:, 0:6 * NT].rearrange("p (j k) -> p j k", j=NT)
                    ag = small[:, 64:64 + 2 * NT].rearrange("p (j k) -> p j k", j=NT)
                    for j in range(NT):
                        last = nc.vector.bn_stats(st[:, j, :], src[:, j, :])
                    then(last)
                    for j in range(NT):
                        last = nc.vector.bn_aggr(ag[:, j, :], st[:, j, :])
                    last.then_inc(stats.sem, 1)
                    dve.wait_ge(rstd_s.sem, b + 1)
                    then(nc.vector.reciprocal(small[:, 96:96 + NT], small[:, 88:88 + NT]))
                    if b >= 2:
                        dve.wait_ge(xn_tr.sem, b - 1)
                    for j in range(NT):
                        last = nc.vector.tensor_scalar(dst[:, j, :], src[:, j, :], ag[:, j, 0:1], small[:, 96 + j:97 + j],
                                                       ALU.subtract, ALU.mult)
                        if j == NT - 1:
                            last.then_inc(xn_ok.sem, 1)
                    dve.wait_ge(xn_ok.sem, b + 1)
                    dve.sem_inc(x_free.sem, 1)
                dve.wait_ge(lin.sem, 1)
                raw = bank(0, 4).rearrange("p (n k) -> p n k", k=16)
                for hp in range(HP):
                    nc.vector.tensor_scalar(la[:, hp * P:(hp + 1) * P], raw[:, :, hp], hc[:, hp:hp + 1], None, ALU.add)
                    last = nc.vector.tensor_copy(be[:, hp * P:(hp + 1) * P], raw[:, :, 8 + hp])
                last.then_inc(zz.sem, 1)
                dve.wait_ge(zz.sem, 1)
                then(nc.vector.tensor_scalar(tmp[0][:], la[:], 0.0, None, ALU.max))
                dve.wait_ge(a_step.sem, 1)
                then(nc.vector.tensor_tensor(tmp[0][:], tmp[0][:], tmp[1][:], ALU.add))
                for hp in range(HP):
                    last = nc.vector.tensor_scalar(la[:, hp * P:(hp + 1) * P], tmp[0][:, hp * P:(hp + 1) * P],
                                                   hc[:, 8 + hp:9 + hp], -1.0, ALU.mult, ALU.mult)
                then(last)
                la4 = la[:].rearrange("p (h c b) -> p h c b", h=HP, c=NC)
                nc.vector.memset(la4[0:1, :, 0, :], RESET)
                then(nc.vector.memset(la4[64:65, :, 0, :], RESET))
                dve.sem_inc(v_step.sem, 1)
                then(nc.vector.tensor_scalar(be[:], be[:], 1.0, None, ALU.add))
                then(nc.vector.reciprocal(tmp[1][:], be[:]))
                then(nc.vector.tensor_scalar(be[:], tmp[1][:], 2.0, None, ALU.mult))
                tp = tabP[:].rearrange("p (n k) -> p n k", k=24)
                tr = tabR[:].rearrange("p (n k) -> p n k", k=16)
                v8 = lambda t: t[:].rearrange("p (n k) -> p n k", k=8)
                nc.vector.tensor_copy(tp[:, :, 0:8], v8(la))
                nc.vector.tensor_scalar(tp[:, :, 8:16], v8(be), -1.0, None, ALU.mult)
                dve.wait_ge(cexp.sem, 1)
                nc.vector.scalar_tensor_tensor(tr[:, :, 0:8], v8(tmp[0]), -1.0, v8(be), ALU.mult, ALU.mult)
                then(nc.vector.memset(S[:], 0.0))
                for n in BD:
                    last = nc.vector.memset(BD[n][:], 0.0)
                then(last)

            @block.scalar
            def _(act):
                act.wait_ge(zeroed.sem, 6)
                for b in range(NB):
                    act.wait_ge(stats.sem, b + 1)
                    ag = small[:, 64:64 + 2 * NT].rearrange("p (j k) -> p j k", j=NT)
                    nc.scalar.activation(small[:, 88:88 + NT], ag[:, :, 1], ACT.Sqrt, bias=eps[:, 0:1]).then_inc(rstd_s.sem, 1)
                    act.wait_ge(xn_tr.sem, b + 1)
                    nc.scalar.activation(xnT3[:, b, HALO:HALO + T], bank(2 * (b % 2), 2), ACT.Copy).then_inc(xn_ev.sem, 1)
                act.preload_act_table_set("natural_log_exp_and_others")
                act.wait_ge(zz.sem, 1)
                steps = [0]

                def then(ins):
                    steps[0] += 1
                    ins.then_inc(rstd_v.sem, 1)
                    act.wait_ge(rstd_v.sem, steps[0])

                then(nc.scalar.activation(tmp[1][:], la[:], ACT.Abs))
                then(nc.scalar.activation(tmp[1][:], tmp[1][:], ACT.Exp, scale=-1.0))
                then(nc.scalar.activation(tmp[1][:], tmp[1][:], ACT.Ln, bias=1.0))
                then(nc.scalar.activation(hc[:, 8:16], hc[:, 8:16], ACT.Exp))
                nc.scalar.activation(be[:], be[:], ACT.Exp, scale=-1.0).then_inc(a_step.sem, 1)
                tp = tabP[:].rearrange("p (n k) -> p n k", k=24)
                tr = tabR[:].rearrange("p (n k) -> p n k", k=16)
                p8 = lambda i: bank(i, 2).rearrange("p (n k) -> p n k", k=8)
                act.wait_ge(cum.sem, 1)
                nc.scalar.activation(tmp[0][:], bank(0, 2), ACT.Exp).then_inc(cexp.sem, 1)
                nc.scalar.activation(tp[:, :, 16:24], p8(2), ACT.Exp)
                nc.scalar.activation(tr[:, :, 8:16], p8(4), ACT.Exp).then_inc(cexp.sem, 1)

            @block.tensor
            def _(pe):
                pe.wait_ge(c_in.sem, C_IN)
                for b in range(NB):
                    pe.wait_ge(xn_ok.sem, b + 1)
                    if b >= 2:
                        pe.wait_ge(xn_ev.sem, b - 1)
                    for j in range(NT):
                        last = nc.tensor.transpose(ps[:, (b % 2) * 1024 + j * P:(b % 2) * 1024 + (j + 1) * P],
                                                   xn[b % 2][:, j * P:(j + 1) * P], ident)
                    last.then_inc(xn_tr.sem, 1)
                pe.wait_ge(xn_ev.sem, NB)
                for c in range(NC):
                    for b in range(NB):
                        for h in range(2):
                            o = (c * NB + b) * 16
                            last = nc.tensor.matmul(ps[64 * h:64 * h + 64, o:o + 16], xnT3[:, b, HALO + c * C:HALO + (c + 1) * C],
                                                    wab_s[:, 16 * h:16 * h + 16], start=True, stop=True)
                last.then_inc(lin.sem, 1)
                pe.wait_ge(v_step.sem, 1)
                for i, o in enumerate((K_LE, K_GT, K_BD)):
                    for k in range(2):
                        last = nc.tensor.matmul(bank(2 * i + k), kc(o), la[:, k * 512:(k + 1) * 512], start=True, stop=True)
                last.then_inc(cum.sem, 1)

        wkq_in = sig("wkq_in", 16)
        wv_in = sig("wv_in", 16)
        st_ok = sig("st_ok")
        lm_ok = sig("lm_ok", 2)
        dec_mm = sig("dec_mm", 3)
        dec_ex = sig("dec_ex", 3)
        dmul = sig("dmul", 2)
        proj = sig("proj", 4)
        tap0 = sig("tap0", 4)
        conv = sig("conv", 12)
        silu = sig("silu", 2)
        silu_v = sig("silu_v", 2)
        sqr = sig("sqr", 2)
        nrm_mm = sig("nrm_mm", 2)
        nrm_mx = sig("nrm_mx", 2)
        nrm_ln = sig("nrm_ln", 2)
        nrm_rn = sig("nrm_rn", 2)
        kb_ok = sig("kb_ok")
        qn_ok = sig("qn_ok")
        qg_ok = sig("qg_ok", 2)
        gram_k = sig("gram_k", 2)
        gram_p = sig("gram_p")
        nd_ok = sig("nd_ok", 2)
        nm_ok = sig("nm_ok", 2)
        pt_ok = sig("pt_ok")
        n_out = sig("n_out", 32)
        n_in = sig("n_in", 16)
        sub = sig("sub", SUBS)
        z_out = sig("z_out", 16)
        z_in = sig("z_in", 32)
        v_tr = sig("v_tr")
        v_ok = sig("v_ok")
        k_tr = sig("k_tr")
        kt_ok = sig("kt_ok")
        x_mm = sig("x_mm", 4)
        x_ok = sig("x_ok", 4)
        y_mm = sig("y_mm", 4)
        y_ok = sig("y_ok", 4)
        z_mm = sig("z_mm", 4)
        z_go = sig("z_go", 4)
        z_ok = sig("z_ok", 4)
        wo_in = sig("wo_in", 16)
        stR_ok = sig("stR_ok")
        ks_mm = sig("ks_mm", 2)
        r_ok = sig("r_ok", 2)
        u_mm = sig("u_mm", 2)
        u_ok = sig("u_ok", 2)
        o_mm = sig("o_mm", 2)
        ds_mm = sig("ds_mm", 2)
        s_ok = sig("s_ok", 2)
        o_sq = sig("o_sq", 2)
        ms_mm = sig("ms_mm", 2)
        ms_ln = sig("ms_ln", 2)
        ms_rn = sig("ms_rn", 2)
        on_ok = sig("on_ok", 2)
        wo_mm = sig("wo_mm")
        acc_ok = sig("acc_ok")

        tabP3 = tabP[:].rearrange("p (n k) -> p n k", k=24)
        tabR3 = tabR[:].rearrange("p (n k) -> p n k", k=16)
        cv4 = cv[:].rearrange("p (i b t) -> p i b t", i=4, b=NB)
        sv4 = sv[:].rearrange("p (b h t) -> p b h t", b=NB, h=2)
        v3 = lambda t, i: t[:, i * 512:(i + 1) * 512].rearrange("p (b t) -> p b t", b=NB)
        pj = bank(0, 2).rearrange("p (b t) -> p b t", b=NB)
        unit = lambda t, b: t[:, b * P:(b + 1) * P]
        half = lambda t, g: t[:, g * 512:(g + 1) * 512]
        LMASK = [k_all[:, K_LV + i * P:K_LV + (i + 1) * P].bitcast(U32) for i in range(2)]
        GROUPS = (range(0, 4), range(4, 8))

        def tap(j, k):
            o = 2 * P + TAPS * (j % 2) + k
            return (w_kq, w_v)[j // 2][:, o:o + 1]

        def first(n):
            return isinstance(n, int) and n == 0

        def pe_proj(pe, n, j):
            if j == 0:
                pe.wait_ge(wkq_in.sem, wkq_in.at(n))
                if not first(n):
                    pe.wait_ge(conv.sem, conv.at(n - 1))
            else:
                pe.wait_ge(conv.sem, conv.at(n, 3 * j))
            if j == 2:
                pe.wait_ge(wv_in.sem, wv_in.at(n))
            if j == 3:
                pe.wait_ge(nd_ok.sem, nd_ok.at(n))
            w = (w_kq, w_v)[j // 2]
            for g in range(2):
                last = nc.tensor.matmul(pj[:, 4 * g:4 * g + 4, 0:CW], w[:, (j % 2) * P:(j % 2 + 1) * P],
                                        xnT3[:, 4 * g:4 * g + 4, bass.ds((n % NC) * C, CW)], start=True, stop=True)
            last.then_inc(proj.sem, 1)

        def pe_decay(pe, n, i):
            if i < 2:
                if not first(n):
                    pe.wait_ge(r_ok.sem, r_ok.at(n - 1, i + 1))
                pe.wait_ge(lm_ok.sem, lm_ok.at(n, i + 1))
            else:
                pe.wait_ge(dec_ex.sem, dec_ex.at(n, 2))
            nc.tensor.matmul(bank((6, 7, 7)[i]), kc((K_LE, K_GT, K_BD)[i]), half(Lm, min(i, 1)),
                             start=True, stop=True).then_inc(dec_mm.sem, 1)

        def pe_norm(pe, n, i):
            pe.wait_ge(sqr.sem, sqr.at(n, i + 1))
            if i:
                pe.wait_ge(dec_ex.sem, dec_ex.at(n, 1))
            elif not first(n):
                pe.wait_ge(v_ok.sem, v_ok.at(n - 1))
            nc.tensor.matmul(bank((4, 6)[i]), kc(K_BD), half(sq, i), start=True, stop=True).then_inc(nrm_mm.sem, 1)

        def pe_gram_k(pe, n):
            pe.wait_ge(kb_ok.sem, kb_ok.at(n))
            pe.wait_ge(conv.sem, conv.at(n, 9))
            for g in range(2):
                for b in GROUPS[g]:
                    last = nc.tensor.matmul(unit(ps, b), unit(BD["KB"], b), unit(BD["KB"], b), start=True, stop=True)
                last.then_inc(gram_k.sem, 1)

        def pe_gram_p(pe, n):
            pe.wait_ge(qn_ok.sem, qn_ok.at(n))
            if not first(n):
                pe.wait_ge(ms_ln.sem, ms_ln.at(n - 1, 1))
            for b in range(NB):
                last = nc.tensor.matmul(ps[:, 2 * 512 + b * C:2 * 512 + (b + 1) * C], unit(BD["KB"], b),
                                        qn[:, b * C:(b + 1) * C], start=True, stop=True)
            last.then_inc(gram_p.sem, 1)

        def pe_ktr(pe, n):
            pe.wait_ge(kb_ok.sem, kb_ok.at(n))
            if not first(n):
                pe.wait_ge(s_ok.sem, s_ok.at(n - 1))
            else:
                pe.wait_ge(dec_ex.sem, dec_ex.at(n))
                pe.wait_ge(nrm_mx.sem, nrm_mx.at(n))
            for b in range(NB):
                last = nc.tensor.transpose(unit(ps, 24 + b), unit(BD["KB"], b), ident)
            last.then_inc(k_tr.sem, 1)

        def pe_vtr(pe, n):
            pe.wait_ge(silu_v.sem, silu_v.at(n))
            if not first(n):
                pe.wait_ge(on_ok.sem, on_ok.at(n - 1))
            for b in range(NB):
                last = nc.tensor.transpose(unit(ps, 16 + b), sv[:, b * P:(b + 1) * P], ident)
            last.then_inc(v_tr.sem, 1)

        def slot(bk, b):
            return ps[:, bk * 512 + (b % 4) * P:bk * 512 + (b % 4 + 1) * P]

        def pe_x(pe, m, l):
            for g in range(2):
                if l == 0:
                    pe.wait_ge(z_in.sem, z_in.at(m))
                    pe.wait_ge(pt_ok.sem, pt_ok.at(m))
                    if not first(m):
                        pe.wait_ge(acc_ok.sem, acc_ok.at(m - 1))
                else:
                    pe.wait_ge(z_ok.sem, z_ok.at(m, g + 1))
                for b in GROUPS[g]:
                    last = nc.tensor.transpose(slot(2 + g, b), unit(BD["Z"], b), ident)
                last.then_inc(x_mm.sem, 1)

        def pe_y(pe, m, l):
            for g in range(2):
                pe.wait_ge(x_ok.sem, x_ok.at(m, 2 * l + g + 1))
                if l == 0:
                    pe.wait_ge(nm_ok.sem, nm_ok.at(m))
                for b in GROUPS[g]:
                    last = nc.tensor.matmul(slot(2 + g, b), unit(BD["NM"], b), unit(BD["Z"], b), start=True, stop=True)
                last.then_inc(y_mm.sem, 1)

        def pe_z(pe, m, n, l):
            if l == 0:
                pe.wait_ge(v_ok.sem, v_ok.at(m))
                if n is not None:
                    pe.wait_ge(nrm_mx.sem, nrm_mx.at(n, 1))
            for g in range(2):
                pe.wait_ge(y_ok.sem, y_ok.at(m, 2 * l + g + 1))
                for b in GROUPS[g]:
                    last = nc.tensor.matmul(slot(4 + g, b), unit(BD["X"], b), unit(BD["Y"], b), start=True, stop=True)
                last.then_inc(z_mm.sem, 1)

        def pe_ks(pe, m):
            pe.wait_ge(kb_ok.sem, kb_ok.at(m))
            pe.wait_ge(kt_ok.sem, kt_ok.at(m))
            if not first(m):
                pe.wait_ge(s_ok.sem, s_ok.at(m - 1))
            for g in range(2):
                for b in GROUPS[g]:
                    last = nc.tensor.matmul(slot(6 + g, b), unit(BD["KB"], b), unit(S, b), start=True, stop=True)
                last.then_inc(ks_mm.sem, 1)

        def pe_u(pe, m, n):
            pe.wait_ge(z_ok.sem, z_ok.at(m))
            pe.wait_ge(r_ok.sem, r_ok.at(m))
            if n is not None:
                pe.wait_ge(nrm_mx.sem, nrm_mx.at(n))
                pe.wait_ge(dec_ex.sem, dec_ex.at(n))
            for g in range(2):
                for b in GROUPS[g]:
                    last = nc.tensor.matmul(slot(6 + g, b), unit(BD["Z"], b), unit(Rr, b), start=True, stop=True)
                last.then_inc(u_mm.sem, 1)

        def pe_o(pe, m):
            pe.wait_ge(qg_ok.sem, qg_ok.at(m))
            pe.wait_ge(pt_ok.sem, pt_ok.at(m))
            for g in range(2):
                pe.wait_ge(u_ok.sem, u_ok.at(m, g + 1))
                for b in GROUPS[g]:
                    nc.tensor.matmul(slot(4 + g, b), unit(S, b), unit(BD["QG"], b), start=True, stop=False)
                    last = nc.tensor.matmul(slot(4 + g, b), unit(U, b), unit(BD["PT"], b), start=False, stop=True)
                last.then_inc(o_mm.sem, 1)

        def pe_ds(pe, m):
            pe.wait_ge(kt_ok.sem, kt_ok.at(m))
            for g in range(2):
                pe.wait_ge(u_ok.sem, u_ok.at(m, g + 1))
                for b in GROUPS[g]:
                    last = nc.tensor.matmul(slot(6 + g, b), unit(BD["KT"], b), unit(U, b), start=True, stop=True)
                last.then_inc(ds_mm.sem, 1)

        def pe_ms(pe, m):
            for g in range(2):
                pe.wait_ge(o_sq.sem, o_sq.at(m, g + 1))
                pe.wait_ge(y_ok.sem, y_ok.at(m, 3 + g))
                nc.tensor.matmul(bank(2 + g), kc(K_ONE), half(oo, g), start=True, stop=True).then_inc(ms_mm.sem, 1)

        def pe_wo(pe, m):
            pe.wait_ge(on_ok.sem, on_ok.at(m))
            pe.wait_ge(wo_in.sem, wo_in.at(m))
            pe.wait_ge(ms_ln.sem, ms_ln.at(m))
            oo4 = oo[:].rearrange("p (b h t) -> p b h t", b=NB, h=2)
            for h in range(2):
                last = nc.tensor.matmul(bank(3), wo_s[:, h * D:(h + 1) * D], oo4[:, :, h, :], start=(h == 0), stop=(h == 1))
            last.then_inc(wo_mm.sem, 1)

        def pe_body(pe, m, n):
            if n is not None:
                pe_proj(pe, n, 0)
            if m is not None and not first(m):
                pe_wo(pe, m - 1)
            if m is not None:
                pe_vtr(pe, m)
                pe_ks(pe, m)
            if n is not None:
                pe_proj(pe, n, 1)
                pe_norm(pe, n, 0)
            if m is not None:
                pe_x(pe, m, 0)
            if n is not None:
                pe_decay(pe, n, 0)
                pe_decay(pe, n, 1)
                pe_proj(pe, n, 2)
            if m is not None:
                pe_y(pe, m, 0)
                pe_z(pe, m, n, 0)
                pe_x(pe, m, 1)
            if n is not None:
                pe_norm(pe, n, 1)
                pe_gram_k(pe, n)
                pe_decay(pe, n, 2)
            if m is not None:
                pe_y(pe, m, 1)
                pe_z(pe, m, n, 1)
            if n is not None:
                pe_proj(pe, n, 3)
            if m is not None:
                pe_u(pe, m, n)
                pe_o(pe, m)
                pe_ds(pe, m)
                pe_ms(pe, m)
            if n is not None:
                pe_gram_p(pe, n)
                pe_ktr(pe, n)
            if n is None:
                pe_wo(pe, m)

        def act_tap0(act, n, j):
            act.wait_ge(proj.sem, proj.at(n, j + 1))
            if not first(n):
                read = (silu, silu_v)[j // 2]
                act.wait_ge(read.sem, read.at(n - 1, j % 2 + 1))
            nc.scalar.activation(cv4[:, j], pj[:, :, 0:C], ACT.Copy, scale=tap(j, 0)).then_inc(tap0.sem, 1)

        def act_exp(act, n, i):
            act.wait_ge(dec_mm.sem, dec_mm.at(n, i + 1))
            if not first(n):
                used = (nd_ok, pt_ok, qg_ok)[i]
                act.wait_ge(used.sem, used.at(n - 1))
            nc.scalar.activation(half(ex, i), bank((6, 7, 7)[i]), ACT.Exp).then_inc(dec_ex.sem, 1)

        def act_silu(act, n, j):
            act.wait_ge(conv.sem, conv.at(n, 3 * j + 3))
            if not first(n):
                act.wait_ge(kb_ok.sem, kb_ok.at(n - 1))
                act.wait_ge(qn_ok.sem, qn_ok.at(n - 1))
            nc.scalar.activation(v3(sl, j), cv4[:, j], ACT.Silu).then_inc(silu.sem, 1)
            if j == 0:
                act.wait_ge(silu.sem, silu.at(n, 1))
                nc.scalar.activation(half(sq, 0), half(sl, 0), ACT.Square).then_inc(sqr.sem, 1)

        def act_silu_v(act, m):
            for h in range(2):
                act.wait_ge(conv.sem, conv.at(m, 9 + 3 * h))
                if not first(m):
                    act.wait_ge(v_tr.sem, v_tr.at(m - 1))
                nc.scalar.activation(sv4[:, :, h, :], cv4[:, 2 + h], ACT.Silu).then_inc(silu_v.sem, 1)

        def act_norm_max(act, n, i):
            act.wait_ge(nrm_mm.sem, nrm_mm.at(n, i + 1))
            nc.scalar.activation(half(sq, i), bank((4, 6)[i]), ACT.Relu, bias=eps[:, 3:4]).then_inc(nrm_mx.sem, 1)

        def act_norm_ln(act, n, i):
            act.wait_ge(nrm_mx.sem, nrm_mx.at(n, i + 1))
            nc.scalar.activation(half(sq, i), half(sq, i), ACT.Ln, bias=eps[:, 2:3]).then_inc(nrm_ln.sem, 1)

        def act_norm(act, n, i):
            act.wait_ge(nrm_ln.sem, nrm_ln.at(n, i + 1))
            nc.scalar.activation(half(sq, i), half(sq, i), ACT.Exp, scale=-0.5).then_inc(nrm_rn.sem, 1)

        def act_v(act, n):
            act.wait_ge(v_tr.sem, v_tr.at(n))
            if not first(n):
                act.wait_ge(r_ok.sem, r_ok.at(n - 1))
            nc.scalar.activation(Vt[:], bank(4, 2), ACT.Copy).then_inc(v_ok.sem, 1)

        def act_x(act, m, l):
            for g in range(2):
                act.wait_ge(x_mm.sem, x_mm.at(m, 2 * l + g + 1))
                nc.scalar.activation(half(BD["X"], g), bank(2 + g), ACT.Copy).then_inc(x_ok.sem, 1)

        def act_y(act, m, l):
            for g in range(2):
                act.wait_ge(y_mm.sem, y_mm.at(m, 2 * l + g + 1))
                nc.scalar.activation(half(BD["Y"], g), bank(2 + g), ACT.Copy).then_inc(y_ok.sem, 1)

        def act_u(act, m):
            for g in range(2):
                act.wait_ge(u_mm.sem, u_mm.at(m, g + 1))
                nc.scalar.activation(half(U, g), bank(6 + g), ACT.Copy).then_inc(u_ok.sem, 1)

        def act_osq(act, m):
            for g in range(2):
                act.wait_ge(o_mm.sem, o_mm.at(m, g + 1))
                if not first(m):
                    act.wait_ge(wo_mm.sem, wo_mm.at(m - 1))
                nc.scalar.activation(half(oo, g), bank(4 + g), ACT.Square).then_inc(o_sq.sem, 1)

        def act_orn(act, m):
            for g in range(2):
                act.wait_ge(ms_mm.sem, ms_mm.at(m, g + 1))
                nc.scalar.activation(half(oo, g), bank(2 + g), ACT.Ln, bias=eps[:, 1:2]).then_inc(ms_ln.sem, 1)
            for g in range(2):
                act.wait_ge(ms_ln.sem, ms_ln.at(m, g + 1))
                nc.scalar.activation(half(oo, g), half(oo, g), ACT.Exp, scale=-0.5).then_inc(ms_rn.sem, 1)

        def act_body(act, m, n):
            if m is not None:
                act_silu_v(act, m)
            if n is not None:
                act_tap0(act, n, 0)
            if m is not None:
                act_v(act, m)
            if n is not None:
                act_silu(act, n, 0)
                act_tap0(act, n, 1)
                act_norm_max(act, n, 0)
            if m is not None:
                act_x(act, m, 0)
            if n is not None:
                act_silu(act, n, 1)
                act_tap0(act, n, 2)
            if m is not None:
                act_y(act, m, 0)
            if n is not None:
                act.preload_act_table_set("natural_log_exp_and_others")
                act_norm_ln(act, n, 0)
                act_exp(act, n, 0)
                act_norm(act, n, 0)
                act_exp(act, n, 1)
            if m is not None:
                act_x(act, m, 1)
            if n is not None:
                act_norm_max(act, n, 1)
                act_exp(act, n, 2)
            if m is not None:
                act_y(act, m, 1)
            if n is not None:
                act_norm_ln(act, n, 1)
                act_tap0(act, n, 3)
                act_norm(act, n, 1)
            if m is not None:
                act_u(act, m)
                act_osq(act, m)
                act_orn(act, m)
            act.preload_act_table_set("silu_and_others")

        def dve_conv(dve, n, j):
            for k in range(1, TAPS):
                if k == 1:
                    dve.wait_ge(tap0.sem, tap0.at(n, j + 1))
                else:
                    dve.wait_ge(conv.sem, conv.at(n, 3 * j + k - 1))
                nc.vector.scalar_tensor_tensor(cv4[:, j], pj[:, :, k:k + C], tap(j, k), cv4[:, j],
                                               ALU.mult, ALU.add).then_inc(conv.sem, 1)

        def dve_keys(dve, n):
            dve.wait_ge(nrm_rn.sem, nrm_rn.at(n, 1))
            if not first(n):
                dve.wait_ge(ks_mm.sem, ks_mm.at(n - 1))
            for a, z in HALF:
                last = nc.vector.tensor_tensor(bd("KB")[a:z, :, a:z], v3(sl, 0)[a:z], v3(sq, 0)[a:z], ALU.mult)
            last.then_inc(kb_ok.sem, 1)

        def dve_n(dve, n):
            if not first(n):
                dve.wait_ge(nm_ok.sem, nm_ok.at(n - 1))
                dve.wait_ge(n_out.sem, n_out.at(n - 1))
            dve.wait_ge(dmul.sem, dmul.at(n, 1))
            gk = bank(0, 2).rearrange("p (b c) -> p b c", b=NB)
            nd = Nd[:].rearrange("p (b t) -> p b t", b=NB)
            for g in range(2):
                dve.wait_ge(gram_k.sem, gram_k.at(n, g + 1))
                for a, z in HALF:
                    last = nc.vector.tensor_tensor(nd[a:z, 4 * g:4 * g + 4, :], gk[a:z, 4 * g:4 * g + 4, a:z],
                                                   v3(ex, 0)[a:z, 4 * g:4 * g + 4, :], ALU.mult)
                last.then_inc(nd_ok.sem, 1)

        def dve_p(dve, n):
            if not first(n):
                dve.wait_ge(o_mm.sem, o_mm.at(n - 1))
            dve.wait_ge(dmul.sem, dmul.at(n, 2))
            dve.wait_ge(gram_p.sem, gram_p.at(n))
            gp = bank(2).rearrange("p (b t) -> p b t", b=NB)
            for a, z in HALF:
                last = nc.vector.tensor_tensor(bd("PT")[a:z, :, a:z], gp[a:z], v3(ex, 1)[a:z], ALU.mult)
            last.then_inc(pt_ok.sem, 1)

        def dve_k(dve, n):
            dve.wait_ge(k_tr.sem, k_tr.at(n))
            dve.wait_ge(st_ok.sem, st_ok.at(n))
            if not first(n):
                dve.wait_ge(ds_mm.sem, ds_mm.at(n - 1))
            for g in range(2):
                last = nc.vector.tensor_tensor(bd("KT")[:, 4 * g:4 * g + 4, :], bank(6 + g).rearrange("p (b c) -> p b c", b=4),
                                               bcast(stP[:, 16:24], P)[:, 4 * g:4 * g + 4, :], ALU.mult)
            last.then_inc(kt_ok.sem, 1)

        blk = lambda t: t[0:64, 0:272].rearrange("g (u w) -> g u w", w=136)[:, :, 0:128].rearrange("g u (k j) -> g u k j", j=16)
        sq16 = lambda t: t[0:64, 0:256].rearrange("g (k j) -> g k j", j=16)
        NB8, XB8, N16, X16 = blk(NS), blk(XT), sq16(NS), sq16(XT)
        prod = tmpS[0:64, 0:512].rearrange("g (a c b) -> g a c b", a=8, c=8)
        WT = tmpW[0:64, 0:64].rearrange("g (c a) -> g c a", c=8)

        def dve_sub(dve, n, lo, hi):
            for k in range(lo, hi):
                if k == 0:
                    dve.wait_ge(n_in.sem, n_in.at(n))
                    if not first(n):
                        dve.wait_ge(z_out.sem, z_out.at(n - 1))
                    dve.wait_ge(c_in.sem, C_IN)
                    ins = nc.vector.tensor_scalar(XB8[:, :, 0, 1:2], NB8[:, :, 1, 0:1], 0.0, None, ALU.add)
                else:
                    dve.wait_ge(sub.sem, sub.at(n, k))
                i = (k + 3) // 2
                t = tmpS[0:64, 0:2 * i * i].rearrange("g (u c j) -> g u c j", u=2, c=i) if i < 8 else None
                if 0 < k < 13 and k % 2:
                    ins = nc.vector.tensor_tensor(t, NB8[:, :, i:i + 1, 0:i].to_broadcast([64, 2, i, i]), XB8[:, :, 0:i, 0:i], ALU.mult)
                elif 0 < k < 13:
                    i = (k + 2) // 2
                    t = tmpS[0:64, 0:2 * i * i].rearrange("g (u c j) -> g u c j", u=2, c=i)
                    ins = nc.vector.tensor_reduce(XB8[:, :, 0:i, i], t, AX, ALU.add)
                elif k == 13:
                    ins = nc.vector.tensor_tensor(prod, N16[:, 8:16, 0:8].rearrange("g a (o b) -> g a o b", o=1).to_broadcast([64, 8, 8, 8]),
                                                  X16[:, 0:8, 0:8].rearrange("g (o c) b -> g o c b", o=1).to_broadcast([64, 8, 8, 8]), ALU.mult)
                elif k == 14:
                    ins = nc.vector.tensor_reduce(WT.rearrange("g c a -> g a c"), prod, AX, ALU.add)
                elif k == 15:
                    ins = nc.vector.tensor_tensor(prod, X16[:, 8:16, 8:16].rearrange("g (o b) a -> g a o b", o=1).to_broadcast([64, 8, 8, 8]),
                                                  WT.rearrange("g (o c) b -> g o c b", o=1).to_broadcast([64, 8, 8, 8]), ALU.mult)
                elif k == 16:
                    ins = nc.vector.tensor_reduce(X16[:, 0:8, 8:16].rearrange("g c a -> g a c"), prod, AX, ALU.add)
                ins.then_inc(sub.sem, 1)

        def dve_z(dve, m, l):
            for g in range(2):
                dve.wait_ge(z_mm.sem, z_mm.at(m, 2 * l + g + 1))
                dve.sem_inc(z_go.sem, 1)
                nc.vector.copy_predicated(bd("Z")[:, 4 * g:4 * g + 4, :], over(LMASK[l], 4, P),
                                          bank(4 + g).rearrange("p (b c) -> p b c", b=4)).then_inc(z_ok.sem, 1)

        def dve_r(dve, m):
            if not first(m):
                dve.wait_ge(s_ok.sem, s_ok.at(m - 1))
            nc.vector.tensor_copy(stR[:].rearrange("p (o k) -> p o k", o=1), tabR3[:, bass.ds(m, 1), :]).then_inc(stR_ok.sem, 1)
            dve.wait_ge(stR_ok.sem, stR_ok.at(m))
            dve.wait_ge(v_ok.sem, v_ok.at(m))
            if not first(m):
                dve.wait_ge(u_mm.sem, u_mm.at(m - 1))
            for g in range(2):
                dve.wait_ge(ks_mm.sem, ks_mm.at(m, g + 1))
                for b in GROUPS[g]:
                    last = nc.vector.scalar_tensor_tensor(unit(Rr, b), slot(6 + g, b), stR[:, b:b + 1], unit(Vt, b), ALU.mult, ALU.add)
                last.then_inc(r_ok.sem, 1)

        def dve_s(dve, m, g):
            dve.wait_ge(o_mm.sem, o_mm.at(m))
            dve.wait_ge(ds_mm.sem, ds_mm.at(m, g + 1))
            for b in GROUPS[g]:
                last = nc.vector.scalar_tensor_tensor(unit(S, b), unit(S, b), stR[:, 8 + b:9 + b], slot(6 + g, b), ALU.mult, ALU.add)
            last.then_inc(s_ok.sem, 1)

        def dve_on(dve, m):
            for g in range(2):
                dve.wait_ge(ms_rn.sem, ms_rn.at(m, g + 1))
                nc.vector.tensor_tensor(half(oo, g), bank(4 + g), half(oo, g), ALU.mult).then_inc(on_ok.sem, 1)

        def dve_acc(dve, m):
            dve.wait_ge(wo_mm.sem, wo_mm.at(m))
            dst = accT3[:, :, bass.ds((m % NC) * C, C)]
            nc.vector.tensor_tensor(dst, bank(3).rearrange("p (b t) -> p b t", b=NB), dst, ALU.add).then_inc(acc_ok.sem, 1)

        def dve_body(dve, m, n):
            if n is not None:
                dve_conv(dve, n, 0)
            if m is not None:
                dve_r(dve, m)
            if m is not None and not first(m):
                dve_acc(dve, m - 1)
            if n is not None:
                dve_conv(dve, n, 1)
                dve_conv(dve, n, 2)
            if m is not None:
                dve_z(dve, m, 0)
            if n is not None:
                dve_keys(dve, n)
                dve_n(dve, n)
            if m is not None:
                dve_z(dve, m, 1)
            if n is not None:
                dve_conv(dve, n, 3)
                dve_sub(dve, n, 0, 14)
            if m is not None:
                dve_s(dve, m, 0)
            if n is not None:
                dve_sub(dve, n, 14, 15)
            if m is not None:
                dve_s(dve, m, 1)
            if n is not None:
                dve_sub(dve, n, 15, SUBS)
            if m is not None:
                dve_on(dve, m)
            if n is not None:
                dve_p(dve, n)
                dve_k(dve, n)
            if n is None:
                dve_acc(dve, m)

        def pool_weights(pool, n):
            if not first(n):
                pool.wait_ge(conv.sem, conv.at(n - 1, 6))
            pool.dma_start(w_kq[:].rearrange("p (o k) -> p o k", o=1), wtab[:, bass.ds(n // NC, 1), 0, :]).then_inc(wkq_in.sem, 16)

        def pool_prepare(pool, m, n):
            pool.wait_ge(cexp.sem, 2)
            if not first(n):
                pool.wait_ge(kt_ok.sem, kt_ok.at(n - 1))
                pool.wait_ge(qg_ok.sem, qg_ok.at(n - 1))
            nc.gpsimd.tensor_copy(stP[:].rearrange("p (o k) -> p o k", o=1), tabP3[:, bass.ds(n, 1), :]).then_inc(st_ok.sem, 1)
            pool.wait_ge(st_ok.sem, st_ok.at(n))
            if not first(n):
                pool.wait_ge(dec_mm.sem, dec_mm.at(n - 1))
            for i, o in enumerate((K_MGT, K_MLE)):
                nc.gpsimd.tensor_tensor(v3(Lm, i), over(kc(o, C), NB, C), bcast(stP[:, 0:8], C), ALU.mult).then_inc(lm_ok.sem, 1)
            pool.wait_ge(silu.sem, silu.at(n))
            nc.gpsimd.tensor_tensor(half(sq, 1), half(sl, 1), half(sl, 1), ALU.mult).then_inc(sqr.sem, 1)
            pool.wait_ge(dec_ex.sem, dec_ex.at(n, 1))
            nc.gpsimd.tensor_tensor(v3(ex, 0), v3(ex, 0), bcast(stP[:, 8:16], C), ALU.mult).then_inc(dmul.sem, 1)
            pool.wait_ge(dec_ex.sem, dec_ex.at(n, 2))
            nc.gpsimd.tensor_tensor(v3(ex, 1), v3(ex, 1), over(kc(K_MLE, C), NB, C), ALU.mult).then_inc(dmul.sem, 1)
            pool.wait_ge(nrm_rn.sem, nrm_rn.at(n, 2))
            if not first(n):
                pool.wait_ge(gram_p.sem, gram_p.at(n - 1))
            nc.gpsimd.tensor_tensor(qn[:], half(sl, 1), half(sq, 1), ALU.mult).then_inc(qn_ok.sem, 1)
            if not first(n):
                pool.wait_ge(y_mm.sem, y_mm.at(n - 1))
            pool.wait_ge(nd_ok.sem, nd_ok.at(n))
            for i, (a, z) in enumerate(HALF):
                if i:
                    pool.wait_ge(nm_ok.sem, nm_ok.at(n, i))
                nc.gpsimd.tensor_tensor(bd("NM")[a:z, :, a:z], Nd[a:z].rearrange("p (b t) -> p b t", b=NB),
                                        over(kc(K_MGT, C), NB, C)[a:z], ALU.mult).then_inc(nm_ok.sem, 1)
            pool.wait_ge(qn_ok.sem, qn_ok.at(n))
            pool.wait_ge(dmul.sem, dmul.at(n))
            pool.wait_ge(dec_ex.sem, dec_ex.at(n, 3))
            if m is not None:
                pool.wait_ge(o_mm.sem, o_mm.at(m))
            for i, (a, z) in enumerate(HALF):
                if i:
                    pool.wait_ge(qg_ok.sem, qg_ok.at(n, i))
                nc.gpsimd.tensor_tensor(bd("QG")[a:z, :, a:z], qn[a:z].rearrange("p (b t) -> p b t", b=NB), v3(ex, 2)[a:z],
                                        ALU.mult).then_inc(qg_ok.sem, 1)

        def pool_body(pool, m, n):
            if n is not None:
                pool_weights(pool, n)
                pool_prepare(pool, m, n)

        rows = lambda s, h: s.rearrange("(b w) -> b w", w=SB)[:, h * 4 * SK:h * 4 * SK + C * C].rearrange("b (r c) -> r b c", c=C)
        blocks = lambda s: s.rearrange("(g w) -> g w", w=SK)[:, 0:16 * C].rearrange("g (i c) -> g i c", c=C)[:, :, 0:16]

        def sp_body(sp, m, n):
            if n is not None:
                if not first(n):
                    sp.wait_ge(conv.sem, conv.at(n - 1))
                sp.dma_start(w_v[:].rearrange("p (o k) -> p o k", o=1), wtab[:, bass.ds(n // NC, 1), 1, :]).then_inc(wv_in.sem, 16)
            if m is not None:
                if not first(m):
                    sp.wait_ge(wo_mm.sem, wo_mm.at(m - 1))
                sp.dma_start(wo_s[:].rearrange("p (o k) -> p o k", o=1), wo[:, bass.ds(m // NC, 1), :]).then_inc(wo_in.sem, 16)
            if n is not None:
                sp.wait_ge(nd_ok.sem, nd_ok.at(n))
                for h, (a, z) in enumerate(HALF):
                    sp.dma_start(rows(scrN, h), Nd[a:z].rearrange("p (b t) -> p b t", b=NB)).then_inc(n_out.sem, 16)
                sp.wait_ge(n_out.sem, n_out.at(n))
                sp.dma_start(N16, blocks(scrN)).then_inc(n_in.sem, 16)
                sp.wait_ge(sub.sem, sub.at(n))
                sp.dma_start(blocks(scrZ), X16).then_inc(z_out.sem, 16)
                sp.wait_ge(z_out.sem, z_out.at(n))
                if m is not None:
                    sp.wait_ge(u_mm.sem, u_mm.at(m))
                for h, (a, z) in enumerate(HALF):
                    sp.dma_start(bd("Z")[a:z, :, a:z], rows(scrZ, h)).then_inc(z_in.sem, 16)

        def program(eng, body):
            body(eng, None, 0)
            body(eng, 0, 1)
            with eng.Fori(1, STEPS - 1) as i:
                body(eng, i, i + 1)
            body(eng, STEPS - 1, None)

        with nc.Block() as block:
            @block.sync
            def _(sp):
                program(sp, sp_body)

            @block.gpsimd
            def _(pool):
                program(pool, pool_body)

            @block.scalar
            def _(act):
                act.preload_act_table_set("silu_and_others")
                program(act, act_body)

            @block.vector
            def _(dve):
                program(dve, dve_body)

            @block.tensor
            def _(pe):
                program(pe, pe_body)

        f_w = sig("f_w")
        f_x = sig("f_x")
        f_at = sig("f_at")
        f_tr = sig("f_tr")
        f_ch = sig("f_ch")
        f_st = sig("f_st", 3)
        f_sd = sig("f_sd", 3)
        f_x1 = sig("f_x1")
        f_n1 = sig("f_n1")
        f_t2 = sig("f_t2")
        f_ev = sig("f_ev")
        f_mx = sig("f_mx")
        f_k = sig("f_k", 2)
        f_rl = sig("f_rl", 2)
        f_sqk = sig("f_sqk")
        f_r = sig("f_r")
        f_sg = sig("f_sg")
        f_v = sig("f_v")
        f_y = sig("f_y")
        f_out = sig("f_out")
        a_s, x_s, x1, n1, hT, dT, xr, xk, ka, rg, yo = (BD["KB"], BD["QG"], BD["PT"], BD["NM"], BD["Z"], BD["X"], BD["Y"], BD["KT"], Vt, Rr, U)
        rl = S
        zc = small[:, 128:129]
        hx = sb("hx", 1 + T)
        wf_s = sb("wf_s", 3 * P)
        out_tok = out.rearrange("b (j p) d -> b p j d", p=P)
        t3 = lambda t: t[:].rearrange("p (j d) -> p j d", j=NT)

        with nc.Block() as block:
            @block.sync
            def _(sp):
                sp.dma_start(wf_s[:], wf).then_inc(f_w.sem, 16)
                for b in range(NB):
                    if b:
                        sp.wait_ge(f_x1.sem, b)
                    sp.dma_start(t3(x_s), x_tok[b]).then_inc(f_x.sem, 16)
                    sp.wait_ge(f_y.sem, b + 1)
                    sp.dma_start(out_tok[b], t3(yo)).then_inc(f_out.sem, 16)
                sp.wait_ge(f_out.sem, 16 * NB)

            @block.gpsimd
            def _(pool):
                nc.gpsimd.memset(hx[:, 0:1], 0.0).then_inc(zeroed.sem, 1)

            @block.vector
            def _(dve):
                chain = [0]

                def then(ins):
                    chain[0] += 1
                    ins.then_inc(f_ch.sem, 1)
                    dve.wait_ge(f_ch.sem, chain[0])

                def norm(src, dst, b, k):
                    st = small[:, 0:6 * NT].rearrange("p (j k) -> p j k", j=NT)
                    ag = small[:, 64:64 + 2 * NT].rearrange("p (j k) -> p j k", j=NT)
                    for j in range(NT):
                        last = nc.vector.bn_stats(st[:, j, :], src[:, j, :])
                    then(last)
                    for j in range(NT):
                        last = nc.vector.bn_aggr(ag[:, j, :], st[:, j, :])
                    last.then_inc(f_st.sem, 1)
                    dve.wait_ge(f_sd.sem, 3 * b + k + 1)
                    then(nc.vector.reciprocal(small[:, 96:96 + NT], small[:, 88:88 + NT]))
                    for j in range(NT):
                        last = nc.vector.tensor_scalar(dst[:, j, :], src[:, j, :], ag[:, j, 0:1], small[:, 96 + j:97 + j],
                                                       ALU.subtract, ALU.mult)
                    then(last)

                for b in range(NB):
                    dve.wait_ge(f_tr.sem, b + 1)
                    norm(bank(0, 2).rearrange("p (j d) -> p j d", j=NT), t3(x1), b, 0)
                    dve.wait_ge(f_x.sem, 16 * (b + 1))
                    then(nc.vector.tensor_tensor(x1[:], x1[:], x_s[:], ALU.add))
                    dve.sem_inc(f_x1.sem, 1)
                    if b:
                        dve.wait_ge(f_t2.sem, b)
                    norm(t3(x1), t3(n1), b, 1)
                    dve.sem_inc(f_n1.sem, 1)
                    dve.wait_ge(f_ev.sem, b + 1)
                    if b:
                        dve.wait_ge(f_r.sem, b)
                    then(nc.vector.tensor_tensor(dT[:], hx[:, 1:1 + T], hx[:, 0:T], ALU.subtract))
                    nc.vector.scalar_tensor_tensor(xr[:], dT[:], muc[:, 0:1], hx[:, 0:T], ALU.mult, ALU.add)
                    then(nc.vector.scalar_tensor_tensor(xk[:], dT[:], muc[:, 1:2], hx[:, 0:T], ALU.mult, ALU.add))
                    dve.sem_inc(f_mx.sem, 1)
                    dve.wait_ge(f_rl.sem, f_rl.at(b))
                    if b:
                        dve.wait_ge(f_v.sem, b)
                    then(nc.vector.tensor_tensor(ka[:], rl[:], rl[:], ALU.mult))
                    dve.sem_inc(f_sqk.sem, 1)
                    dve.wait_ge(f_v.sem, b + 1)
                    dve.wait_ge(f_sg.sem, b + 1)
                    if b:
                        dve.wait_ge(f_out.sem, 16 * b)
                    then(nc.vector.tensor_tensor(rg[:], bank(4, 2), rg[:], ALU.mult))
                    norm(t3(rg), t3(yo), b, 2)
                    then(nc.vector.tensor_tensor(yo[:], yo[:], x1[:], ALU.add))
                    dve.sem_inc(f_y.sem, 1)

            @block.scalar
            def _(act):
                def root(b, k):
                    act.wait_ge(f_st.sem, 3 * b + k + 1)
                    ag = small[:, 64:64 + 2 * NT].rearrange("p (j k) -> p j k", j=NT)
                    nc.scalar.activation(small[:, 88:88 + NT], ag[:, :, 1], ACT.Sqrt, bias=eps[:, 0:1]).then_inc(f_sd.sem, 1)

                for b in range(NB):
                    if b:
                        act.wait_ge(f_tr.sem, b)
                    nc.scalar.activation(a_s[:], accT3[:, b, :], ACT.Copy).then_inc(f_at.sem, 1)
                    root(b, 0)
                    root(b, 1)
                    act.wait_ge(f_t2.sem, b + 1)
                    if b:
                        act.wait_ge(f_mx.sem, b)
                    nc.scalar.activation(hx[:, 1:1 + T], bank(2, 2), ACT.Copy).then_inc(f_ev.sem, 1)
                    for k in range(2):
                        act.wait_ge(f_k.sem, 2 * b + k + 1)
                        if b:
                            act.wait_ge(f_sqk.sem, b)
                        nc.scalar.activation(rl[:, k * 512:(k + 1) * 512], bank(k), ACT.Relu).then_inc(f_rl.sem, 1)
                    act.wait_ge(f_r.sem, b + 1)
                    if b:
                        act.wait_ge(f_y.sem, b)
                    nc.scalar.activation(rg[:], bank(2, 2), ACT.Sigmoid).then_inc(f_sg.sem, 1)
                    root(b, 2)

            @block.tensor
            def _(pe):
                pe.wait_ge(zeroed.sem, 7)
                pe.wait_ge(f_w.sem, 16)
                for b in range(NB):
                    pe.wait_ge(f_at.sem, b + 1)
                    if b:
                        pe.wait_ge(f_rl.sem, f_rl.at(b - 1))
                    for j in range(NT):
                        last = nc.tensor.transpose(unit(ps, j), unit(a_s, j), ident)
                    last.then_inc(f_tr.sem, 1)
                    pe.wait_ge(f_n1.sem, b + 1)
                    if b:
                        pe.wait_ge(f_sg.sem, b)
                    for j in range(NT):
                        last = nc.tensor.transpose(unit(ps, 8 + j), unit(n1, j), ident)
                    last.then_inc(f_t2.sem, 1)
                    pe.wait_ge(f_mx.sem, b + 1)
                    for k in range(2):
                        nc.tensor.matmul(bank(k), wf_s[:, P:2 * P], xk[:, k * 512:(k + 1) * 512], start=True, stop=True).then_inc(f_k.sem, 1)
                    for j in range(NT):
                        last = nc.tensor.matmul(unit(ps, 8 + j), unit(xr, j), wf_s[:, 0:P], start=True, stop=True)
                    last.then_inc(f_r.sem, 1)
                    pe.wait_ge(f_sqk.sem, b + 1)
                    if b:
                        pe.wait_ge(f_y.sem, b)
                    for j in range(NT):
                        last = nc.tensor.matmul(unit(ps, 16 + j), unit(ka, j), wf_s[:, 2 * P:3 * P], start=True, stop=True)
                    last.then_inc(f_v.sem, 1)


def kernel(L0_attn_x, L0_attn_Wq, L0_attn_Wk, L0_attn_Wv, L0_attn_Wb, L0_attn_Wa, L0_attn_A_log, L0_attn_dt_bias,
           L0_attn_Wo, L0_attn_conv_q, L0_attn_conv_k, L0_attn_conv_v, L0_ffn_W_r, L0_ffn_W_k, L0_ffn_W_v,
           L0_ffn_mu_r, L0_ffn_mu_k):
    import concourse.bacc as bacc
    from concourse.bass_utils import run_bass_kernel_spmd

    f = lambda a: np.asarray(a)
    wk = f(L0_attn_Wk).reshape(HP, P, D)
    wq = f(L0_attn_Wq).reshape(HP, P, D)
    wv = f(L0_attn_Wv).reshape(HP, 2, P, D)
    w = np.stack([wk, wq, wv[:, 0], wv[:, 1]], 1)
    w = w.transpose(3, 0, 1, 2).reshape(D, HP, 2, 2 * P)
    ck = f(L0_attn_conv_k).reshape(HP, P, TAPS)
    cq = f(L0_attn_conv_q).reshape(HP, P, TAPS)
    cvw = f(L0_attn_conv_v).reshape(HP, 2, P, TAPS)
    taps = np.stack([ck, cq, cvw[:, 0], cvw[:, 1]], 1).transpose(2, 0, 1, 3).reshape(P, HP, 2, 2 * TAPS)
    wtab = np.concatenate([w, taps], 3)
    wo = f(L0_attn_Wo).reshape(D, HP, 2, DV).transpose(3, 1, 2, 0).reshape(DV, HP, 2 * D)
    wa = f(L0_attn_Wa).reshape(HP, 2, D).transpose(2, 1, 0)
    wb = f(L0_attn_Wb).reshape(HP, 2, D).transpose(2, 1, 0)
    wab = np.concatenate([wa, wb], 2).reshape(D, 32)
    col = lambda a: np.repeat(f(a).reshape(HP, 2).T, C, axis=0)
    hcol = np.concatenate([col(L0_attn_dt_bias), col(L0_attn_A_log)], 1)
    wf = np.concatenate([f(L0_ffn_W_r).T, f(L0_ffn_W_k).T, f(L0_ffn_W_v).T], 1)
    mu = np.stack([f(L0_ffn_mu_r), f(L0_ffn_mu_k)], 1)
    arrays = {"x": f(L0_attn_x), "wtab": wtab, "wo": wo, "wab": wab, "hcol": hcol, "cst": constants(), "wf": wf, "mu": mu}
    arrays = {k: np.ascontiguousarray(v) for k, v in arrays.items()}
    nc = bacc.Bacc("TRN2", target_bir_lowering=False, num_devices=1)
    args = [nc.dram_tensor(k, v.shape, mybir.dt.from_np(v.dtype), kind="ExternalInput").ap() for k, v in arrays.items()]
    out = nc.dram_tensor("out", (NB, T, D), F32, kind="ExternalOutput").ap()
    build(nc, *args, out)
    r = run_bass_kernel_spmd(nc, [arrays], core_ids=[0])
    return r.results[0]["out"]
```

```python
import numpy as np
import concourse.bass as bass
from concourse import mybir
from contextlib import ExitStack

F32 = mybir.dt.float32
ALU = mybir.AluOpType
ACT = mybir.ActivationFunctionType

P = 128
NB = 8
T = 1024
D = 128
H = 16
HP = H // 2
DK = 64
DV = 128
C = 64
NC = T // C
STEPS = HP * NC
TAPS = 4
HALO = TAPS - 1
CW = C + HALO
NT = T // P
SUBS = 18
SK = 16 * C + 16
SB = NB * SK
C_IN = 80
HALF = ((0, 64), (64, 128))
RESET = -1.0e4
EPS_LN = 1e-5
EPS_L2 = 1e-6
EPS_RMS = 1e-6

K_ID, K_LE, K_GT, K_BD, K_ONE, K_MGT, K_MLE, K_XI = 0, 128, 256, 384, 512, 640, 704, 768
K_N = K_XI + 272


def constants():
    c = np.zeros((P, K_N), np.float32)
    i = np.arange(P)
    same = (i[:, None] // C) == (i[None, :] // C)
    r, t = (i % C)[:, None], (i % C)[None, :]
    c[:, K_ID:K_ID + P] = np.eye(P)
    c[:, K_LE:K_LE + P] = same & (r <= t)
    c[:, K_GT:K_GT + P] = same & (r > t)
    c[:, K_BD:K_BD + P] = same
    c[:, K_ONE:K_ONE + P] = 1.0 / DV
    j = np.arange(C)[None, :]
    c[:, K_MGT:K_MGT + C] = r > j
    c[:, K_MLE:K_MLE + C] = r <= j
    c[:, K_XI:K_XI + 256:17] = 1.0
    return c


class Signal:

    def __init__(self, sem, per):
        self.sem, self.per = sem, per

    def at(self, step, k=None):
        return step * self.per + (self.per if k is None else k)


AX = mybir.AxisListType.X


def build(nc, x, wtab, wo, wab, hcol, cst, wf, mu, out):
    with ExitStack() as ctx:
        def sb(name, cols, dt=F32):
            return ctx.enter_context(nc.sbuf_tensor(name, [P, cols], dt))

        def sig(name, per=1):
            return Signal(ctx.enter_context(nc.semaphore(name)), per)

        k_all = sb("k_all", K_N)
        xnT = sb("xnT", NB * (HALO + T))
        accT = sb("accT", NB * T)
        tabP = sb("tabP", STEPS * 24)
        tabR = sb("tabR", STEPS * 16)
        xnT3 = xnT[:].rearrange("p (b t) -> p b t", b=NB)
        accT3 = accT[:].rearrange("p (b t) -> p b t", b=NB)
        w_kq = sb("w_kq", 2 * P + 2 * TAPS)
        w_v = sb("w_v", 2 * P + 2 * TAPS)
        wo_s = sb("wo_s", 2 * D)
        stP = sb("stP", 24)
        stR = sb("stR", 16)
        Lm = sb("Lm", 2 * 512)
        ex = sb("ex", 3 * 512)
        cv = sb("cv", 4 * 512)
        sl = sb("sl", 2 * 512)
        sv = sb("sv", 1024)
        sq = sb("sq", 2 * 512)
        qn = sb("qn", 512)
        BD = {n: sb(n, NB * P) for n in ("KB", "QG", "PT", "NM", "Z", "X0", "X", "Y", "KT")}
        Vt = sb("Vt", NB * P)
        Rr = sb("Rr", NB * P)
        U = sb("U", NB * P)
        S = sb("S", NB * P)
        oo = sb("oo", 1024)
        Nd = sb("Nd", 512)
        NS = sb("NS", 272)
        XT = sb("XT", 272)
        XB = sb("XB", 256)
        tmpS = sb("tmpS", 512)
        tmpW = sb("tmpW", 64)
        scrN = nc.dram_tensor("scrN", (NB * SB,), F32, kind="Internal").ap()
        scrZ = nc.dram_tensor("scrZ", (NB * SB,), F32, kind="Internal").ap()
        scrX = nc.dram_tensor("scrX", (NB * SB,), F32, kind="Internal").ap()
        eps = sb("eps", 4)
        small = sb("small", 256)
        hc = sb("hc", 16)
        muc = sb("muc", 2)

        def bd(n):
            return BD[n][:].rearrange("p (b c) -> p b c", b=NB)

        ps = ctx.enter_context(nc.psum_tensor("ps", [P, 8 * 512], F32))

        def bank(i, n=1):
            return ps[:, i * 512:(i + n) * 512]

        def kc(o, n=P):
            return k_all[:, o:o + n]

        ident = kc(K_ID)
        unit = lambda t, b: t[:, b * P:(b + 1) * P]

        def bcast(ap, n):
            return ap.rearrange("p (b o) -> p b o", o=1).to_broadcast([P, NB, n])

        def over(ap, b, n):
            return ap.rearrange("p (o n) -> p o n", o=1).to_broadcast([P, b, n])

        c_in = sig("c_in")
        xt_in = [sig("xt_in0"), sig("xt_in1")]
        x_free = sig("x_free")
        zeroed = sig("zeroed")
        scr_z = sig("scr_z")
        bd_zero = sig("bd_zero")
        stats = sig("stats")
        rstd_s = sig("rstd_s")
        rstd_v = sig("rstd_v")
        xn_ok = sig("xn_ok")
        xn_tr = sig("xn_tr")
        xn_ev = sig("xn_ev")
        dchain = sig("dchain")
        lin = sig("lin")
        zz = sig("zz")
        a_step = sig("a_step")
        v_step = sig("v_step")
        cum = sig("cum")
        cexp = sig("cexp")

        xt = [KBuf for KBuf in (BD["KB"], BD["QG"])]
        xn = [BD["PT"], BD["NM"]]
        wab_s = cv[:, 0:32]
        la = Vt
        be = Rr
        tmp = [U, S]
        x_tok = x.rearrange("b (j p) d -> b p j d", p=P)
        pairs = [(b // 2, b % 2) for b in range(NB)]

        with nc.Block() as block:
            @block.sync
            def _(sp):
                sp.dma_start(k_all[:], cst).then_inc(c_in.sem, 16)
                sp.dma_start(wab_s, wab).then_inc(c_in.sem, 16)
                sp.dma_start(hc[:], hcol).then_inc(c_in.sem, 16)
                sp.dma_start(muc[:], mu).then_inc(c_in.sem, 16)
                sp.dma_start(XT[:], cst[:, K_XI:K_XI + 272]).then_inc(c_in.sem, 16)
                for b in range(NB):
                    if b >= 2:
                        sp.wait_ge(x_free.sem, b - 1)
                    sp.dma_start(xt[b % 2][:].rearrange("p (j d) -> p j d", j=NT), x_tok[b]).then_inc(xt_in[b % 2].sem, 16)

            @block.gpsimd
            def _(pool):
                nc.gpsimd.memset(eps[:, 0:1], EPS_LN).then_inc(zeroed.sem, 1)
                nc.gpsimd.memset(eps[:, 1:2], EPS_RMS).then_inc(zeroed.sem, 1)
                nc.gpsimd.memset(eps[:, 2:3], EPS_L2 * EPS_L2).then_inc(zeroed.sem, 1)
                nc.gpsimd.memset(eps[:, 3:4], -EPS_L2 * EPS_L2).then_inc(zeroed.sem, 1)
                nc.gpsimd.memset(xnT3[:, :, 0:HALO], 0.0).then_inc(zeroed.sem, 1)
                nc.gpsimd.memset(accT[:], 0.0).then_inc(zeroed.sem, 1)
                for n in ("Z", "X0", "X", "Y", "KT"):
                    nc.gpsimd.memset(BD[n][:], 0.0).then_inc(bd_zero.sem, 1)
                pool.wait_ge(zeroed.sem, 6)
                for scr in (scrZ, scrX):
                    pool.dma_start(scr.rearrange("(p k) -> p k", p=P), accT[:, 0:NB * SB // P]).then_inc(scr_z.sem, 16)
                pool.wait_ge(scr_z.sem, 32)
                pool.wait_ge(xn_tr.sem, NB)
                for n in ("KB", "QG", "PT", "NM"):
                    nc.gpsimd.memset(BD[n][:], 0.0).then_inc(bd_zero.sem, 1)
                pool.wait_ge(bd_zero.sem, len(BD))

            @block.vector
            def _(dve):
                chain = [0]

                def then(ins):
                    chain[0] += 1
                    ins.then_inc(dchain.sem, 1)
                    dve.wait_ge(dchain.sem, chain[0])

                for b in range(NB):
                    src = xt[b % 2][:].rearrange("p (j d) -> p j d", j=NT)
                    dst = xn[b % 2][:].rearrange("p (j d) -> p j d", j=NT)
                    dve.wait_ge(xt_in[b % 2].sem, 16 * (b // 2 + 1))
                    st = small[:, 0:6 * NT].rearrange("p (j k) -> p j k", j=NT)
                    ag = small[:, 64:64 + 2 * NT].rearrange("p (j k) -> p j k", j=NT)
                    for j in range(NT):
                        last = nc.vector.bn_stats(st[:, j, :], src[:, j, :])
                    then(last)
                    for j in range(NT):
                        last = nc.vector.bn_aggr(ag[:, j, :], st[:, j, :])
                    last.then_inc(stats.sem, 1)
                    dve.wait_ge(rstd_s.sem, b + 1)
                    then(nc.vector.reciprocal(small[:, 96:96 + NT], small[:, 88:88 + NT]))
                    if b >= 2:
                        dve.wait_ge(xn_tr.sem, b - 1)
                    for j in range(NT):
                        last = nc.vector.tensor_scalar(dst[:, j, :], src[:, j, :], ag[:, j, 0:1], small[:, 96 + j:97 + j],
                                                       ALU.subtract, ALU.mult)
                        if j == NT - 1:
                            last.then_inc(xn_ok.sem, 1)
                    dve.wait_ge(xn_ok.sem, b + 1)
                    dve.sem_inc(x_free.sem, 1)
                dve.wait_ge(lin.sem, 1)
                raw = bank(0, 4).rearrange("p (n k) -> p n k", k=16)
                for hp in range(HP):
                    nc.vector.tensor_scalar(la[:, hp * P:(hp + 1) * P], raw[:, :, hp], hc[:, hp:hp + 1], None, ALU.add)
                    last = nc.vector.tensor_copy(be[:, hp * P:(hp + 1) * P], raw[:, :, 8 + hp])
                last.then_inc(zz.sem, 1)
                dve.wait_ge(zz.sem, 1)
                then(nc.vector.tensor_scalar(tmp[0][:], la[:], 0.0, None, ALU.max))
                dve.wait_ge(a_step.sem, 1)
                then(nc.vector.tensor_tensor(tmp[0][:], tmp[0][:], tmp[1][:], ALU.add))
                for hp in range(HP):
                    last = nc.vector.tensor_scalar(la[:, hp * P:(hp + 1) * P], tmp[0][:, hp * P:(hp + 1) * P],
                                                   hc[:, 8 + hp:9 + hp], -1.0, ALU.mult, ALU.mult)
                then(last)
                la4 = la[:].rearrange("p (h c b) -> p h c b", h=HP, c=NC)
                nc.vector.memset(la4[0:1, :, 0, :], RESET)
                then(nc.vector.memset(la4[64:65, :, 0, :], RESET))
                dve.sem_inc(v_step.sem, 1)
                then(nc.vector.tensor_scalar(be[:], be[:], 1.0, None, ALU.add))
                then(nc.vector.reciprocal(tmp[1][:], be[:]))
                then(nc.vector.tensor_scalar(be[:], tmp[1][:], 2.0, None, ALU.mult))
                tp = tabP[:].rearrange("p (n k) -> p n k", k=24)
                tr = tabR[:].rearrange("p (n k) -> p n k", k=16)
                v8 = lambda t: t[:].rearrange("p (n k) -> p n k", k=8)
                nc.vector.tensor_copy(tp[:, :, 0:8], v8(la))
                nc.vector.tensor_scalar(tp[:, :, 8:16], v8(be), -1.0, None, ALU.mult)
                dve.wait_ge(cexp.sem, 1)
                nc.vector.scalar_tensor_tensor(tr[:, :, 0:8], v8(tmp[0]), -1.0, v8(be), ALU.mult, ALU.mult)
                dve.wait_ge(cexp.sem, 1)
                then(nc.vector.memset(S[:], 0.0))

            @block.scalar
            def _(act):
                act.wait_ge(zeroed.sem, 6)
                for b in range(NB):
                    act.wait_ge(stats.sem, b + 1)
                    ag = small[:, 64:64 + 2 * NT].rearrange("p (j k) -> p j k", j=NT)
                    nc.scalar.activation(small[:, 88:88 + NT], ag[:, :, 1], ACT.Sqrt, bias=eps[:, 0:1]).then_inc(rstd_s.sem, 1)
                    act.wait_ge(xn_tr.sem, b + 1)
                    nc.scalar.activation(xnT3[:, b, HALO:HALO + T], bank(4 + 2 * (b % 2), 2), ACT.Copy).then_inc(xn_ev.sem, 1)
                act.preload_act_table_set("natural_log_exp_and_others")
                act.wait_ge(zz.sem, 1)
                steps = [0]

                def then(ins):
                    steps[0] += 1
                    ins.then_inc(rstd_v.sem, 1)
                    act.wait_ge(rstd_v.sem, steps[0])

                then(nc.scalar.activation(tmp[1][:], la[:], ACT.Abs))
                then(nc.scalar.activation(tmp[1][:], tmp[1][:], ACT.Exp, scale=-1.0))
                then(nc.scalar.activation(tmp[1][:], tmp[1][:], ACT.Ln, bias=1.0))
                then(nc.scalar.activation(hc[:, 8:16], hc[:, 8:16], ACT.Exp))
                nc.scalar.activation(be[:], be[:], ACT.Exp, scale=-1.0).then_inc(a_step.sem, 1)
                tp = tabP[:].rearrange("p (n k) -> p n k", k=24)
                tr = tabR[:].rearrange("p (n k) -> p n k", k=16)
                p8 = lambda i: bank(i, 2).rearrange("p (n k) -> p n k", k=8)
                act.wait_ge(cum.sem, 1)
                nc.scalar.activation(tmp[0][:], bank(0, 2), ACT.Exp).then_inc(cexp.sem, 1)
                nc.scalar.activation(tp[:, :, 16:24], p8(2), ACT.Exp)
                nc.scalar.activation(tr[:, :, 8:16], p8(4), ACT.Exp).then_inc(cexp.sem, 1)

            @block.tensor
            def _(pe):
                pe.wait_ge(c_in.sem, C_IN)
                for b in range(NB + 1):
                    if b < NB:
                        pe.wait_ge(xn_ok.sem, b + 1)
                        if b >= 2:
                            pe.wait_ge(xn_ev.sem, b - 1)
                        for j in range(NT):
                            last = nc.tensor.transpose(unit(ps, 16 + 8 * (b % 2) + j), unit(xn[b % 2], j), ident)
                        last.then_inc(xn_tr.sem, 1)
                    if b:
                        pe.wait_ge(xn_ev.sem, b)
                        for c in range(NC):
                            for h in range(2):
                                o = (c * NB + b - 1) * 16
                                last = nc.tensor.matmul(ps[64 * h:64 * h + 64, o:o + 16],
                                                        xnT3[:, b - 1, HALO + c * C:HALO + (c + 1) * C],
                                                        wab_s[:, 16 * h:16 * h + 16], start=True, stop=True)
                last.then_inc(lin.sem, 1)
                pe.wait_ge(v_step.sem, 1)
                for i, o in enumerate((K_LE, K_GT, K_BD)):
                    for k in range(2):
                        last = nc.tensor.matmul(bank(2 * i + k), kc(o), la[:, k * 512:(k + 1) * 512], start=True, stop=True)
                last.then_inc(cum.sem, 1)

        wkq_in = sig("wkq_in", 16)
        wv_in = sig("wv_in", 16)
        st_ok = sig("st_ok")
        lm_ok = sig("lm_ok", 2)
        dec_mm = sig("dec_mm", 3)
        dec_ex = sig("dec_ex", 3)
        dmul = sig("dmul", 2)
        proj = sig("proj", 4)
        tap0 = sig("tap0", 4)
        conv = sig("conv", 12)
        silu = sig("silu", 2)
        silu_v = sig("silu_v", 2)
        sqr = sig("sqr", 2)
        nrm_mm = sig("nrm_mm", 2)
        nrm_mx = sig("nrm_mx", 2)
        nrm_ln = sig("nrm_ln", 2)
        nrm_rn = sig("nrm_rn", 2)
        kb_ok = sig("kb_ok")
        qn_ok = sig("qn_ok")
        qg_ok = sig("qg_ok", 2)
        gram_k = sig("gram_k", 2)
        gram_p = sig("gram_p")
        nd_ok = sig("nd_ok", 2)
        nm_ok = sig("nm_ok", 2)
        pt_ok = sig("pt_ok")
        n_out = sig("n_out", 32)
        n_in = sig("n_in", 16)
        sub = sig("sub", SUBS)
        z_out = sig("z_out", 16)
        z_in = sig("z_in", 32)
        x_out = sig("x_out", 16)
        x_in = sig("x_in", 32)
        v_tr = sig("v_tr")
        v_ok = sig("v_ok")
        k_tr = sig("k_tr")
        kt_ok = sig("kt_ok")
        x_mm = sig("x_mm", 2)
        x_ok = sig("x_ok", 2)
        y_mm = sig("y_mm", 4)
        y_ok = sig("y_ok", 4)
        z_mm = sig("z_mm", 4)
        z_ok = sig("z_ok", 2)
        wo_in = sig("wo_in", 16)
        stR_ok = sig("stR_ok")
        ks_mm = sig("ks_mm", 2)
        r_ok = sig("r_ok", 2)
        u_mm = sig("u_mm", 2)
        u_ok = sig("u_ok", 2)
        o_mm = sig("o_mm", 2)
        ds_mm = sig("ds_mm", 2)
        s_ok = sig("s_ok", 2)
        o_sq = sig("o_sq", 2)
        ms_mm = sig("ms_mm", 2)
        ms_ln = sig("ms_ln", 2)
        ms_rn = sig("ms_rn", 2)
        on_ok = sig("on_ok", 2)
        wo_mm = sig("wo_mm")
        acc_ok = sig("acc_ok")

        tabP3 = tabP[:].rearrange("p (n k) -> p n k", k=24)
        tabR3 = tabR[:].rearrange("p (n k) -> p n k", k=16)
        cv4 = cv[:].rearrange("p (i b t) -> p i b t", i=4, b=NB)
        sv4 = sv[:].rearrange("p (b h t) -> p b h t", b=NB, h=2)
        v3 = lambda t, i: t[:, i * 512:(i + 1) * 512].rearrange("p (b t) -> p b t", b=NB)
        pj = bank(0, 2).rearrange("p (b t) -> p b t", b=NB)
        half = lambda t, g: t[:, g * 512:(g + 1) * 512]
        GROUPS = (range(0, 4), range(4, 8))

        def tap(j, k):
            o = 2 * P + TAPS * (j % 2) + k
            return (w_kq, w_v)[j // 2][:, o:o + 1]

        def first(n):
            return isinstance(n, int) and n == 0

        def pe_proj(pe, n, j):
            if j == 0:
                pe.wait_ge(wkq_in.sem, wkq_in.at(n))
                if not first(n):
                    pe.wait_ge(conv.sem, conv.at(n - 1))
            else:
                pe.wait_ge(conv.sem, conv.at(n, 3 * j))
            if j == 2:
                pe.wait_ge(wv_in.sem, wv_in.at(n))
            if j == 3:
                pe.wait_ge(nd_ok.sem, nd_ok.at(n))
            w = (w_kq, w_v)[j // 2]
            for g in range(2):
                last = nc.tensor.matmul(pj[:, 4 * g:4 * g + 4, 0:CW], w[:, (j % 2) * P:(j % 2 + 1) * P],
                                        xnT3[:, 4 * g:4 * g + 4, bass.ds((n % NC) * C, CW)], start=True, stop=True)
            last.then_inc(proj.sem, 1)

        def pe_decay(pe, n, i):
            if i < 2:
                if not first(n):
                    pe.wait_ge(r_ok.sem, r_ok.at(n - 1, i + 1))
                pe.wait_ge(lm_ok.sem, lm_ok.at(n, i + 1))
            else:
                pe.wait_ge(dec_ex.sem, dec_ex.at(n, 2))
            nc.tensor.matmul(bank((6, 7, 7)[i]), kc((K_LE, K_GT, K_BD)[i]), half(Lm, min(i, 1)),
                             start=True, stop=True).then_inc(dec_mm.sem, 1)

        def pe_norm(pe, n, i):
            pe.wait_ge(sqr.sem, sqr.at(n, i + 1))
            if i:
                pe.wait_ge(dec_ex.sem, dec_ex.at(n, 1))
            elif not first(n):
                pe.wait_ge(v_ok.sem, v_ok.at(n - 1))
            nc.tensor.matmul(bank((4, 6)[i]), kc(K_BD), half(sq, i), start=True, stop=True).then_inc(nrm_mm.sem, 1)

        def pe_gram_k(pe, n):
            pe.wait_ge(kb_ok.sem, kb_ok.at(n))
            pe.wait_ge(conv.sem, conv.at(n, 9))
            for g in range(2):
                for b in GROUPS[g]:
                    last = nc.tensor.matmul(unit(ps, b), unit(BD["KB"], b), unit(BD["KB"], b), start=True, stop=True)
                last.then_inc(gram_k.sem, 1)

        def pe_gram_p(pe, n):
            pe.wait_ge(qn_ok.sem, qn_ok.at(n))
            if not first(n):
                pe.wait_ge(ms_ln.sem, ms_ln.at(n - 1, 1))
            for b in range(NB):
                last = nc.tensor.matmul(ps[:, 2 * 512 + b * C:2 * 512 + (b + 1) * C], unit(BD["KB"], b),
                                        qn[:, b * C:(b + 1) * C], start=True, stop=True)
            last.then_inc(gram_p.sem, 1)

        def pe_ktr(pe, n):
            pe.wait_ge(kb_ok.sem, kb_ok.at(n))
            if not first(n):
                pe.wait_ge(s_ok.sem, s_ok.at(n - 1))
            else:
                pe.wait_ge(dec_ex.sem, dec_ex.at(n))
                pe.wait_ge(nrm_mx.sem, nrm_mx.at(n))
            for b in range(NB):
                last = nc.tensor.transpose(unit(ps, 24 + b), unit(BD["KB"], b), ident)
            last.then_inc(k_tr.sem, 1)

        def pe_vtr(pe, n):
            pe.wait_ge(silu_v.sem, silu_v.at(n))
            if not first(n):
                pe.wait_ge(on_ok.sem, on_ok.at(n - 1))
            for b in range(NB):
                last = nc.tensor.transpose(unit(ps, 16 + b), sv[:, b * P:(b + 1) * P], ident)
            last.then_inc(v_tr.sem, 1)

        def slot(bk, b):
            return ps[:, bk * 512 + (b % 4) * P:bk * 512 + (b % 4 + 1) * P]

        def pe_x(pe, m):
            pe.wait_ge(z_ok.sem, z_ok.at(m, 1))
            for g in range(2):
                for b in GROUPS[g]:
                    last = nc.tensor.transpose(slot(2 + g, b), unit(BD["Z"], b), ident)
                last.then_inc(x_mm.sem, 1)

        def pe_y(pe, m, l):
            for g in range(2):
                if l:
                    pe.wait_ge(x_ok.sem, x_ok.at(m, g + 1))
                else:
                    pe.wait_ge(z_in.sem, z_in.at(m))
                    pe.wait_ge(nm_ok.sem, nm_ok.at(m))
                    pe.wait_ge(pt_ok.sem, pt_ok.at(m))
                    if g == 1 and not first(m):
                        pe.wait_ge(acc_ok.sem, acc_ok.at(m - 1))
                for b in GROUPS[g]:
                    last = nc.tensor.matmul(slot(2 + g, b), unit(BD["NM"], b), unit(BD["Z"], b), start=True, stop=True)
                last.then_inc(y_mm.sem, 1)

        def pe_z(pe, m, n, l):
            if l == 0:
                pe.wait_ge(v_ok.sem, v_ok.at(m))
                pe.wait_ge(x_in.sem, x_in.at(m))
                if n is not None:
                    pe.wait_ge(nrm_mx.sem, nrm_mx.at(n, 1))
            for g in range(2):
                pe.wait_ge(y_ok.sem, y_ok.at(m, 2 * l + g + 1))
                for b in GROUPS[g]:
                    last = nc.tensor.matmul(slot(4 + g, b), unit(BD["X" if l else "X0"], b), unit(BD["Y"], b), start=True, stop=True)
                last.then_inc(z_mm.sem, 1)

        def pe_ks(pe, m):
            pe.wait_ge(kb_ok.sem, kb_ok.at(m))
            pe.wait_ge(kt_ok.sem, kt_ok.at(m))
            if not first(m):
                pe.wait_ge(s_ok.sem, s_ok.at(m - 1))
            for g in range(2):
                for b in GROUPS[g]:
                    last = nc.tensor.matmul(slot(6 + g, b), unit(BD["KB"], b), unit(S, b), start=True, stop=True)
                last.then_inc(ks_mm.sem, 1)

        def pe_u(pe, m, n):
            pe.wait_ge(z_ok.sem, z_ok.at(m))
            pe.wait_ge(r_ok.sem, r_ok.at(m))
            if n is not None:
                pe.wait_ge(nrm_mx.sem, nrm_mx.at(n))
                pe.wait_ge(dec_ex.sem, dec_ex.at(n))
            for g in range(2):
                for b in GROUPS[g]:
                    last = nc.tensor.matmul(slot(6 + g, b), unit(BD["Z"], b), unit(Rr, b), start=True, stop=True)
                last.then_inc(u_mm.sem, 1)

        def pe_o(pe, m):
            pe.wait_ge(qg_ok.sem, qg_ok.at(m))
            pe.wait_ge(pt_ok.sem, pt_ok.at(m))
            for g in range(2):
                pe.wait_ge(u_ok.sem, u_ok.at(m, g + 1))
                for b in GROUPS[g]:
                    nc.tensor.matmul(slot(4 + g, b), unit(S, b), unit(BD["QG"], b), start=True, stop=False)
                    last = nc.tensor.matmul(slot(4 + g, b), unit(U, b), unit(BD["PT"], b), start=False, stop=True)
                last.then_inc(o_mm.sem, 1)

        def pe_ds(pe, m):
            pe.wait_ge(kt_ok.sem, kt_ok.at(m))
            for g in range(2):
                pe.wait_ge(u_ok.sem, u_ok.at(m, g + 1))
                for b in GROUPS[g]:
                    last = nc.tensor.matmul(slot(6 + g, b), unit(BD["KT"], b), unit(U, b), start=True, stop=True)
                last.then_inc(ds_mm.sem, 1)

        def pe_ms(pe, m):
            for g in range(2):
                pe.wait_ge(o_sq.sem, o_sq.at(m, g + 1))
                pe.wait_ge(y_ok.sem, y_ok.at(m, 3 + g))
                nc.tensor.matmul(bank(2 + g), kc(K_ONE), half(oo, g), start=True, stop=True).then_inc(ms_mm.sem, 1)

        def pe_wo(pe, m):
            pe.wait_ge(on_ok.sem, on_ok.at(m))
            pe.wait_ge(wo_in.sem, wo_in.at(m))
            pe.wait_ge(ms_ln.sem, ms_ln.at(m))
            oo4 = oo[:].rearrange("p (b h t) -> p b h t", b=NB, h=2)
            for h in range(2):
                last = nc.tensor.matmul(bank(3), wo_s[:, h * D:(h + 1) * D], oo4[:, :, h, :], start=(h == 0), stop=(h == 1))
            last.then_inc(wo_mm.sem, 1)

        def pe_body(pe, m, n):
            if m is not None:
                pe_vtr(pe, m)
            if n is not None:
                pe_proj(pe, n, 0)
            if m is not None and not first(m):
                pe_wo(pe, m - 1)
            if m is not None:
                pe_ks(pe, m)
            if n is not None:
                pe_proj(pe, n, 1)
                pe_norm(pe, n, 0)
            if m is not None:
                pe_y(pe, m, 0)
                pe_z(pe, m, n, 0)
            if n is not None:
                pe_decay(pe, n, 0)
                pe_proj(pe, n, 2)
                pe_decay(pe, n, 1)
            if m is not None:
                pe_x(pe, m)
            if n is not None:
                pe_norm(pe, n, 1)
            if m is not None:
                pe_y(pe, m, 1)
            if n is not None:
                pe_decay(pe, n, 2)
                pe_gram_k(pe, n)
            if m is not None:
                pe_z(pe, m, n, 1)
            if n is not None:
                pe_proj(pe, n, 3)
            if m is not None:
                pe_u(pe, m, n)
                pe_o(pe, m)
                pe_ds(pe, m)
                pe_ms(pe, m)
            if n is not None:
                pe_gram_p(pe, n)
                pe_ktr(pe, n)
            if n is None:
                pe_wo(pe, m)

        def act_tap0(act, n, j):
            act.wait_ge(proj.sem, proj.at(n, j + 1))
            if not first(n):
                read = (silu, silu_v)[j // 2]
                act.wait_ge(read.sem, read.at(n - 1, j % 2 + 1))
            nc.scalar.activation(cv4[:, j], pj[:, :, 0:C], ACT.Copy, scale=tap(j, 0)).then_inc(tap0.sem, 1)

        def act_exp(act, n, i):
            act.wait_ge(dec_mm.sem, dec_mm.at(n, i + 1))
            if not first(n):
                used = (nd_ok, pt_ok, qg_ok)[i]
                act.wait_ge(used.sem, used.at(n - 1))
            nc.scalar.activation(half(ex, i), bank((6, 7, 7)[i]), ACT.Exp).then_inc(dec_ex.sem, 1)

        def act_silu(act, n, j):
            act.wait_ge(conv.sem, conv.at(n, 3 * j + 3))
            if not first(n):
                act.wait_ge(kb_ok.sem, kb_ok.at(n - 1))
                act.wait_ge(qn_ok.sem, qn_ok.at(n - 1))
            nc.scalar.activation(v3(sl, j), cv4[:, j], ACT.Silu).then_inc(silu.sem, 1)
            if j == 0:
                act.wait_ge(silu.sem, silu.at(n, 1))
                nc.scalar.activation(half(sq, 0), half(sl, 0), ACT.Square).then_inc(sqr.sem, 1)

        def act_silu_v(act, m):
            for h in range(2):
                act.wait_ge(conv.sem, conv.at(m, 9 + 3 * h))
                if not first(m):
                    act.wait_ge(v_tr.sem, v_tr.at(m - 1))
                nc.scalar.activation(sv4[:, :, h, :], cv4[:, 2 + h], ACT.Silu).then_inc(silu_v.sem, 1)

        def act_norm_max(act, n, i):
            act.wait_ge(nrm_mm.sem, nrm_mm.at(n, i + 1))
            nc.scalar.activation(half(sq, i), bank((4, 6)[i]), ACT.Relu, bias=eps[:, 3:4]).then_inc(nrm_mx.sem, 1)

        def act_norm_ln(act, n, i):
            act.wait_ge(nrm_mx.sem, nrm_mx.at(n, i + 1))
            nc.scalar.activation(half(sq, i), half(sq, i), ACT.Ln, bias=eps[:, 2:3]).then_inc(nrm_ln.sem, 1)

        def act_norm(act, n, i):
            act.wait_ge(nrm_ln.sem, nrm_ln.at(n, i + 1))
            nc.scalar.activation(half(sq, i), half(sq, i), ACT.Exp, scale=-0.5).then_inc(nrm_rn.sem, 1)

        def act_v(act, n):
            act.wait_ge(v_tr.sem, v_tr.at(n))
            if not first(n):
                act.wait_ge(r_ok.sem, r_ok.at(n - 1))
            nc.scalar.activation(Vt[:], bank(4, 2), ACT.Copy).then_inc(v_ok.sem, 1)

        def act_x(act, m):
            for g in range(2):
                act.wait_ge(x_mm.sem, x_mm.at(m, g + 1))
                nc.scalar.activation(half(BD["X"], g), bank(2 + g), ACT.Copy).then_inc(x_ok.sem, 1)

        def act_y(act, m, l, groups=(0, 1)):
            for g in groups:
                act.wait_ge(y_mm.sem, y_mm.at(m, 2 * l + g + 1))
                nc.scalar.activation(half(BD["Y"], g), bank(2 + g), ACT.Copy).then_inc(y_ok.sem, 1)

        def act_z(act, m):
            act.wait_ge(z_mm.sem, z_mm.at(m))
            zp = bank(4, 2).rearrange("p (b c) -> p b c", b=NB)
            for r in range(0, P, 64):
                last = nc.scalar.activation(bd("Z")[r:r + 32, :, r + 32:r + 64], zp[r:r + 32, :, r + 32:r + 64], ACT.Copy)
            last.then_inc(z_ok.sem, 1)

        def act_u(act, m):
            for g in range(2):
                act.wait_ge(u_mm.sem, u_mm.at(m, g + 1))
                nc.scalar.activation(half(U, g), bank(6 + g), ACT.Copy).then_inc(u_ok.sem, 1)

        def act_osq(act, m):
            for g in range(2):
                act.wait_ge(o_mm.sem, o_mm.at(m, g + 1))
                if not first(m):
                    act.wait_ge(wo_mm.sem, wo_mm.at(m - 1))
                nc.scalar.activation(half(oo, g), bank(4 + g), ACT.Square).then_inc(o_sq.sem, 1)

        def act_orn(act, m):
            for g in range(2):
                act.wait_ge(ms_mm.sem, ms_mm.at(m, g + 1))
                nc.scalar.activation(half(oo, g), bank(2 + g), ACT.Ln, bias=eps[:, 1:2]).then_inc(ms_ln.sem, 1)
            for g in range(2):
                act.wait_ge(ms_ln.sem, ms_ln.at(m, g + 1))
                nc.scalar.activation(half(oo, g), half(oo, g), ACT.Exp, scale=-0.5).then_inc(ms_rn.sem, 1)

        def act_body(act, m, n):
            if m is not None:
                act_silu_v(act, m)
            if n is not None:
                act_tap0(act, n, 0)
            if m is not None:
                act_v(act, m)
            if n is not None:
                act_silu(act, n, 0)
                act_tap0(act, n, 1)
                act_norm_max(act, n, 0)
            if m is not None:
                act_y(act, m, 0)
            if n is not None:
                act_silu(act, n, 1)
                act.preload_act_table_set("natural_log_exp_and_others")
                act_norm_ln(act, n, 0)
                act_tap0(act, n, 2)
                act_exp(act, n, 0)
                act_exp(act, n, 1)
            if m is not None:
                act_x(act, m)
            if n is not None:
                act_norm(act, n, 0)
                act_norm_max(act, n, 1)
            if m is not None:
                act_y(act, m, 1, (0,))
            if n is not None:
                act_norm_ln(act, n, 1)
                act_exp(act, n, 2)
            if m is not None:
                act_y(act, m, 1, (1,))
                act_z(act, m)
            if n is not None:
                act_tap0(act, n, 3)
            if m is not None:
                act_u(act, m)
            if n is not None:
                act_norm(act, n, 1)
            if m is not None:
                act_osq(act, m)
                act_orn(act, m)
            act.preload_act_table_set("silu_and_others")

        def dve_conv(dve, n, j, lo=1, hi=TAPS):
            for k in range(lo, hi):
                if k == 1:
                    dve.wait_ge(tap0.sem, tap0.at(n, j + 1))
                else:
                    dve.wait_ge(conv.sem, conv.at(n, 3 * j + k - 1))
                nc.vector.scalar_tensor_tensor(cv4[:, j], pj[:, :, k:k + C], tap(j, k), cv4[:, j],
                                               ALU.mult, ALU.add).then_inc(conv.sem, 1)

        def dve_keys(dve, n):
            dve.wait_ge(nrm_rn.sem, nrm_rn.at(n, 1))
            if not first(n):
                dve.wait_ge(ks_mm.sem, ks_mm.at(n - 1))
            for a, z in HALF:
                last = nc.vector.tensor_tensor(bd("KB")[a:z, :, a:z], v3(sl, 0)[a:z], v3(sq, 0)[a:z], ALU.mult)
            last.then_inc(kb_ok.sem, 1)

        def dve_n(dve, n):
            if not first(n):
                dve.wait_ge(nm_ok.sem, nm_ok.at(n - 1))
                dve.wait_ge(n_out.sem, n_out.at(n - 1))
            dve.wait_ge(dmul.sem, dmul.at(n, 1))
            gk = bank(0, 2).rearrange("p (b c) -> p b c", b=NB)
            nd = Nd[:].rearrange("p (b t) -> p b t", b=NB)
            for g in range(2):
                dve.wait_ge(gram_k.sem, gram_k.at(n, g + 1))
                for a, z in HALF:
                    last = nc.vector.tensor_tensor(nd[a:z, 4 * g:4 * g + 4, :], gk[a:z, 4 * g:4 * g + 4, a:z],
                                                   v3(ex, 0)[a:z, 4 * g:4 * g + 4, :], ALU.mult)
                last.then_inc(nd_ok.sem, 1)

        def dve_p(dve, n):
            if not first(n):
                dve.wait_ge(o_mm.sem, o_mm.at(n - 1))
            dve.wait_ge(dmul.sem, dmul.at(n, 2))
            dve.wait_ge(gram_p.sem, gram_p.at(n))
            gp = bank(2).rearrange("p (b t) -> p b t", b=NB)
            for a, z in HALF:
                last = nc.vector.tensor_tensor(bd("PT")[a:z, :, a:z], gp[a:z], v3(ex, 1)[a:z], ALU.mult)
            last.then_inc(pt_ok.sem, 1)

        def dve_k(dve, n):
            dve.wait_ge(k_tr.sem, k_tr.at(n))
            dve.wait_ge(st_ok.sem, st_ok.at(n))
            if not first(n):
                dve.wait_ge(ds_mm.sem, ds_mm.at(n - 1))
            for g in range(2):
                last = nc.vector.tensor_tensor(bd("KT")[:, 4 * g:4 * g + 4, :], bank(6 + g).rearrange("p (b c) -> p b c", b=4),
                                               bcast(stP[:, 16:24], P)[:, 4 * g:4 * g + 4, :], ALU.mult)
            last.then_inc(kt_ok.sem, 1)

        blk = lambda t: t[0:64, 0:272].rearrange("g (u w) -> g u w", w=136)[:, :, 0:128].rearrange("g u (k j) -> g u k j", j=16)
        sq16 = lambda t: t[0:64, 0:256].rearrange("g (k j) -> g k j", j=16)
        NB8, XB8, N16, X16 = blk(NS), blk(XT), sq16(NS), sq16(XT)
        prod = tmpS[0:64, 0:512].rearrange("g (a c b) -> g a c b", a=8, c=8)
        WT = tmpW[0:64, 0:64].rearrange("g (c a) -> g c a", c=8)

        def dve_sub(dve, n, lo, hi):
            for k in range(lo, hi):
                if k == 0:
                    dve.wait_ge(n_in.sem, n_in.at(n))
                    if not first(n):
                        dve.wait_ge(z_out.sem, z_out.at(n - 1))
                    dve.wait_ge(c_in.sem, C_IN)
                    ins = nc.vector.tensor_scalar(XB8[:, :, 0, 1:2], NB8[:, :, 1, 0:1], 0.0, None, ALU.add)
                else:
                    dve.wait_ge(sub.sem, sub.at(n, k))
                i = (k + 3) // 2
                t = tmpS[0:64, 0:2 * i * i].rearrange("g (u c j) -> g u c j", u=2, c=i) if i < 8 else None
                if 0 < k < 13 and k % 2:
                    ins = nc.vector.tensor_tensor(t, NB8[:, :, i:i + 1, 0:i].to_broadcast([64, 2, i, i]), XB8[:, :, 0:i, 0:i], ALU.mult)
                elif 0 < k < 13:
                    i = (k + 2) // 2
                    t = tmpS[0:64, 0:2 * i * i].rearrange("g (u c j) -> g u c j", u=2, c=i)
                    ins = nc.vector.tensor_reduce(XB8[:, :, 0:i, i], t, AX, ALU.add)
                elif k == 13:
                    ins = nc.vector.tensor_tensor(prod, N16[:, 8:16, 0:8].rearrange("g a (o b) -> g a o b", o=1).to_broadcast([64, 8, 8, 8]),
                                                  X16[:, 0:8, 0:8].rearrange("g (o c) b -> g o c b", o=1).to_broadcast([64, 8, 8, 8]), ALU.mult)
                elif k == 14:
                    ins = nc.vector.tensor_reduce(WT.rearrange("g c a -> g a c"), prod, AX, ALU.add)
                elif k == 15:
                    ins = nc.vector.tensor_tensor(prod, X16[:, 8:16, 8:16].rearrange("g (o b) a -> g a o b", o=1).to_broadcast([64, 8, 8, 8]),
                                                  WT.rearrange("g (o c) b -> g o c b", o=1).to_broadcast([64, 8, 8, 8]), ALU.mult)
                elif k == 17:
                    if not first(n):
                        dve.wait_ge(x_out.sem, x_out.at(n - 1))
                    ins = nc.vector.tensor_copy(XB[0:64, :].rearrange("g (j k) -> g j k", j=16), X16.rearrange("g k j -> g j k"))
                elif k == 16:
                    ins = nc.vector.tensor_reduce(X16[:, 0:8, 8:16].rearrange("g c a -> g a c"), prod, AX, ALU.add)
                ins.then_inc(sub.sem, 1)

        def dve_z(dve, m):
            dve.wait_ge(z_mm.sem, z_mm.at(m, 2))
            zp = bank(4, 2).rearrange("p (b c) -> p b c", b=NB)
            for r in range(0, P, 32):
                last = nc.vector.tensor_copy(bd("Z")[r:r + 16, :, r + 16:r + 32], zp[r:r + 16, :, r + 16:r + 32])
            last.then_inc(z_ok.sem, 1)

        def dve_r(dve, m):
            if not first(m):
                dve.wait_ge(s_ok.sem, s_ok.at(m - 1))
            nc.vector.tensor_copy(stR[:].rearrange("p (o k) -> p o k", o=1), tabR3[:, bass.ds(m, 1), :]).then_inc(stR_ok.sem, 1)
            dve.wait_ge(stR_ok.sem, stR_ok.at(m))
            dve.wait_ge(v_ok.sem, v_ok.at(m))
            if not first(m):
                dve.wait_ge(u_mm.sem, u_mm.at(m - 1))
            for g in range(2):
                dve.wait_ge(ks_mm.sem, ks_mm.at(m, g + 1))
                for b in GROUPS[g]:
                    last = nc.vector.scalar_tensor_tensor(unit(Rr, b), slot(6 + g, b), stR[:, b:b + 1], unit(Vt, b), ALU.mult, ALU.add)
                last.then_inc(r_ok.sem, 1)

        def dve_s(dve, m, g):
            dve.wait_ge(o_mm.sem, o_mm.at(m))
            dve.wait_ge(ds_mm.sem, ds_mm.at(m, g + 1))
            for b in GROUPS[g]:
                last = nc.vector.scalar_tensor_tensor(unit(S, b), unit(S, b), stR[:, 8 + b:9 + b], slot(6 + g, b), ALU.mult, ALU.add)
            last.then_inc(s_ok.sem, 1)

        def dve_on(dve, m, groups=(0, 1)):
            for g in groups:
                dve.wait_ge(ms_rn.sem, ms_rn.at(m, g + 1))
                nc.vector.tensor_tensor(half(oo, g), bank(4 + g), half(oo, g), ALU.mult).then_inc(on_ok.sem, 1)

        def dve_acc(dve, m):
            dve.wait_ge(wo_mm.sem, wo_mm.at(m))
            dst = accT3[:, :, bass.ds((m % NC) * C, C)]
            nc.vector.tensor_tensor(dst, bank(3).rearrange("p (b t) -> p b t", b=NB), dst, ALU.add).then_inc(acc_ok.sem, 1)

        def dve_body(dve, m, n):
            if n is not None:
                dve_conv(dve, n, 0)
            if m is not None:
                dve_r(dve, m)
            if m is not None and not first(m):
                dve_acc(dve, m - 1)
            if n is not None:
                dve_conv(dve, n, 1)
            if m is not None:
                dve_z(dve, m)
            if n is not None:
                dve_conv(dve, n, 2)
                dve_keys(dve, n)
                dve_n(dve, n)
                dve_conv(dve, n, 3)
                dve_sub(dve, n, 0, 10)
            if m is not None:
                dve_s(dve, m, 0)
            if n is not None:
                dve_sub(dve, n, 10, 14)
            if m is not None:
                dve_s(dve, m, 1)
            if n is not None:
                dve_sub(dve, n, 14, 15)
            if m is not None:
                dve_on(dve, m)
            if n is not None:
                dve_sub(dve, n, 15, 17)
                dve_p(dve, n)
                dve_sub(dve, n, 17, SUBS)
                dve_k(dve, n)
            if n is None:
                dve_acc(dve, m)

        def pool_weights(pool, n):
            if not first(n):
                pool.wait_ge(conv.sem, conv.at(n - 1, 6))
            pool.dma_start(w_kq[:].rearrange("p (o k) -> p o k", o=1), wtab[:, bass.ds(n // NC, 1), 0, :]).then_inc(wkq_in.sem, 16)

        def pool_prepare(pool, m, n):
            pool.wait_ge(cexp.sem, 2)
            if not first(n):
                pool.wait_ge(kt_ok.sem, kt_ok.at(n - 1))
                pool.wait_ge(qg_ok.sem, qg_ok.at(n - 1))
            nc.gpsimd.tensor_copy(stP[:].rearrange("p (o k) -> p o k", o=1), tabP3[:, bass.ds(n, 1), :]).then_inc(st_ok.sem, 1)
            pool.wait_ge(st_ok.sem, st_ok.at(n))
            if not first(n):
                pool.wait_ge(dec_mm.sem, dec_mm.at(n - 1))
            for i, o in enumerate((K_MGT, K_MLE)):
                nc.gpsimd.tensor_tensor(v3(Lm, i), over(kc(o, C), NB, C), bcast(stP[:, 0:8], C), ALU.mult).then_inc(lm_ok.sem, 1)
            pool.wait_ge(silu.sem, silu.at(n))
            nc.gpsimd.tensor_tensor(half(sq, 1), half(sl, 1), half(sl, 1), ALU.mult).then_inc(sqr.sem, 1)
            pool.wait_ge(dec_ex.sem, dec_ex.at(n, 1))
            nc.gpsimd.tensor_tensor(v3(ex, 0), v3(ex, 0), bcast(stP[:, 8:16], C), ALU.mult).then_inc(dmul.sem, 1)
            pool.wait_ge(dec_ex.sem, dec_ex.at(n, 2))
            nc.gpsimd.tensor_tensor(v3(ex, 1), v3(ex, 1), over(kc(K_MLE, C), NB, C), ALU.mult).then_inc(dmul.sem, 1)
            pool.wait_ge(nrm_rn.sem, nrm_rn.at(n, 2))
            if not first(n):
                pool.wait_ge(gram_p.sem, gram_p.at(n - 1))
            nc.gpsimd.tensor_tensor(qn[:], half(sl, 1), half(sq, 1), ALU.mult).then_inc(qn_ok.sem, 1)
            if not first(n):
                pool.wait_ge(y_mm.sem, y_mm.at(n - 1))
            pool.wait_ge(nd_ok.sem, nd_ok.at(n))
            for i, (a, z) in enumerate(HALF):
                if i:
                    pool.wait_ge(nm_ok.sem, nm_ok.at(n, i))
                nc.gpsimd.tensor_tensor(bd("NM")[a:z, :, a:z], Nd[a:z].rearrange("p (b t) -> p b t", b=NB),
                                        over(kc(K_MGT, C), NB, C)[a:z], ALU.mult).then_inc(nm_ok.sem, 1)
            pool.wait_ge(qn_ok.sem, qn_ok.at(n))
            pool.wait_ge(dmul.sem, dmul.at(n))
            pool.wait_ge(dec_ex.sem, dec_ex.at(n, 3))
            if m is not None:
                pool.wait_ge(o_mm.sem, o_mm.at(m))
            for i, (a, z) in enumerate(HALF):
                if i:
                    pool.wait_ge(qg_ok.sem, qg_ok.at(n, i))
                nc.gpsimd.tensor_tensor(bd("QG")[a:z, :, a:z], qn[a:z].rearrange("p (b t) -> p b t", b=NB), v3(ex, 2)[a:z],
                                        ALU.mult).then_inc(qg_ok.sem, 1)

        def pool_body(pool, m, n):
            if n is not None:
                pool_weights(pool, n)
                pool_prepare(pool, m, n)

        rows = lambda s, h: s.rearrange("(b w) -> b w", w=SB)[:, h * 4 * SK:h * 4 * SK + C * C].rearrange("b (r c) -> r b c", c=C)
        blocks = lambda s: s.rearrange("(g w) -> g w", w=SK)[:, 0:16 * C].rearrange("g (i c) -> g i c", c=C)[:, :, 0:16]

        def sp_body(sp, m, n):
            if n is not None:
                if not first(n):
                    sp.wait_ge(conv.sem, conv.at(n - 1))
                sp.dma_start(w_v[:].rearrange("p (o k) -> p o k", o=1), wtab[:, bass.ds(n // NC, 1), 1, :]).then_inc(wv_in.sem, 16)
            if m is not None:
                if not first(m):
                    sp.wait_ge(wo_mm.sem, wo_mm.at(m - 1))
                sp.dma_start(wo_s[:].rearrange("p (o k) -> p o k", o=1), wo[:, bass.ds(m // NC, 1), :]).then_inc(wo_in.sem, 16)
            if n is not None:
                sp.wait_ge(nd_ok.sem, nd_ok.at(n))
                for h, (a, z) in enumerate(HALF):
                    sp.dma_start(rows(scrN, h), Nd[a:z].rearrange("p (b t) -> p b t", b=NB)).then_inc(n_out.sem, 16)
                sp.wait_ge(n_out.sem, n_out.at(n))
                sp.dma_start(N16, blocks(scrN)).then_inc(n_in.sem, 16)
                sp.wait_ge(sub.sem, sub.at(n, SUBS - 1))
                sp.dma_start(blocks(scrZ), X16).then_inc(z_out.sem, 16)
                sp.wait_ge(sub.sem, sub.at(n))
                sp.dma_start(blocks(scrX), XB[0:64, :].rearrange("g (k j) -> g k j", j=16)).then_inc(x_out.sem, 16)
                sp.wait_ge(z_out.sem, z_out.at(n))
                if m is not None:
                    sp.wait_ge(u_mm.sem, u_mm.at(m))
                for h, (a, z) in enumerate(HALF):
                    sp.dma_start(bd("Z")[a:z, :, a:z], rows(scrZ, h)).then_inc(z_in.sem, 16)
                sp.wait_ge(x_out.sem, x_out.at(n))
                if m is not None:
                    sp.wait_ge(z_mm.sem, z_mm.at(m, 2))
                for h, (a, z) in enumerate(HALF):
                    sp.dma_start(bd("X0")[a:z, :, a:z], rows(scrX, h)).then_inc(x_in.sem, 16)

        def program(eng, body):
            body(eng, None, 0)
            body(eng, 0, 1)
            with eng.Fori(1, STEPS - 1) as i:
                body(eng, i, i + 1)
            body(eng, STEPS - 1, None)

        with nc.Block() as block:
            @block.sync
            def _(sp):
                program(sp, sp_body)

            @block.gpsimd
            def _(pool):
                program(pool, pool_body)

            @block.scalar
            def _(act):
                act.preload_act_table_set("silu_and_others")
                program(act, act_body)

            @block.vector
            def _(dve):
                program(dve, dve_body)

            @block.tensor
            def _(pe):
                program(pe, pe_body)

        f_w = sig("f_w")
        f_zc = sig("f_zc")
        f_x = [sig("f_x0"), sig("f_x1")]
        f_out = [sig("f_out0"), sig("f_out1")]
        f_tr = sig("f_tr")
        f_st = [sig("f_st0"), sig("f_st1"), sig("f_st2")]
        f_sd = [sig("f_sd0"), sig("f_sd1"), sig("f_sd2")]
        f_nb = sig("f_nb")
        f_n0 = sig("f_n0")
        f_r1 = sig("f_r1")
        f_n1 = sig("f_n1")
        f_t1 = sig("f_t1")
        f_ev = sig("f_ev")
        f_wm = sig("f_wm")
        f_k = sig("f_k")
        f_rl = sig("f_rl")
        f_ka = sig("f_ka")
        f_r = sig("f_r")
        f_sg = sig("f_sg")
        f_v = sig("f_v")
        f_rg = sig("f_rg")
        f_n2 = sig("f_n2")
        f_y = sig("f_y")
        f_ch = sig("f_ch")
        x_s = (BD["KB"], BD["QG"])
        x1 = (BD["PT"], BD["NM"], BD["X0"])
        yo = (BD["Z"], BD["X"])
        n1, ka, sg, rg = BD["Y"], U, S, oo
        hx = cv[:, 0:1 + T]
        wf_s = sq[:, 0:3 * P]
        wm = [sq[:, 384 + k * P:384 + (k + 1) * P] for k in range(4)]
        out_tok = out.rearrange("b (j p) d -> b p j d", p=P)
        t3 = lambda t: t[:].rearrange("p (j d) -> p j d", j=NT)
        st = [small[:, 48 * k:48 * k + 6 * NT].rearrange("p (j k) -> p j k", j=NT) for k in range(3)]
        ag = [small[:, 144 + 16 * k:160 + 16 * k].rearrange("p (j k) -> p j k", j=NT) for k in range(3)]
        sd = [small[:, 192 + 8 * k:200 + 8 * k] for k in range(3)]
        rs = [small[:, 216 + 8 * k:224 + 8 * k] for k in range(3)]
        nb = small[:, 240:248]
        mu1 = small[:, 248:250]

        with nc.Block() as block:
            @block.sync
            def _(sp):
                sp.dma_start(wf_s, wf).then_inc(f_w.sem, 16)
                for b in range(2):
                    sp.dma_start(t3(x_s[b]), x_tok[b]).then_inc(f_x[b].sem, 16)
                for b in range(NB):
                    if b + 2 < NB:
                        sp.wait_ge(f_r1.sem, b + 1)
                        sp.dma_start(t3(x_s[b % 2]), x_tok[b + 2]).then_inc(f_x[b % 2].sem, 16)
                    sp.wait_ge(f_y.sem, b + 1)
                    sp.dma_start(out_tok[b], t3(yo[b % 2])).then_inc(f_out[b % 2].sem, 16)
                for k in range(2):
                    sp.wait_ge(f_out[k].sem, 16 * (NB // 2))

            @block.gpsimd
            def _(pool):
                nc.gpsimd.memset(hx[:, 0:1], 0.0).then_inc(f_zc.sem, 1)
                for i in range(NB + 2):
                    if i < NB:
                        pool.wait_ge(f_n0.sem, i + 1)
                        pool.wait_ge(f_x[i % 2].sem, 16 * (i // 2 + 1))
                        nc.gpsimd.tensor_tensor(x1[i % 3][:], x1[i % 3][:], x_s[i % 2][:], ALU.add).then_inc(f_r1.sem, 1)
                    if i >= 2:
                        b = i - 2
                        pool.wait_ge(f_n2.sem, b + 1)
                        nc.gpsimd.tensor_tensor(yo[b % 2][:], yo[b % 2][:], x1[b % 3][:], ALU.add).then_inc(f_y.sem, 1)

            @block.vector
            def _(dve):
                chain = [0]

                def then(ins):
                    chain[0] += 1
                    ins.then_inc(f_ch.sem, 1)
                    dve.wait_ge(f_ch.sem, chain[0])

                def stats(src, k):
                    for j in range(NT):
                        last = nc.vector.bn_stats(st[k][:, j, :], src[:, j, :])
                    then(last)
                    for j in range(NT):
                        last = nc.vector.bn_aggr(ag[k][:, j, :], st[k][:, j, :])
                    last.then_inc(f_st[k].sem, 1)

                def norm(src, dst, k, done):
                    for j in range(NT):
                        last = nc.vector.tensor_scalar(dst[:, j, :], src[:, j, :], ag[k][:, j, 0:1], rs[k][:, j:j + 1],
                                                       ALU.subtract, ALU.mult)
                    last.then_inc(done.sem, 1)

                dve.wait_ge(f_w.sem, 16)
                then(nc.vector.tensor_scalar(mu1, muc[:], -1.0, 1.0, ALU.mult, ALU.add))
                for k in range(2):
                    nc.vector.tensor_scalar(wm[2 * k], wf_s[:, k * P:(k + 1) * P], muc[:, k:k + 1], None, ALU.mult)
                    last = nc.vector.tensor_scalar(wm[2 * k + 1], wf_s[:, k * P:(k + 1) * P], mu1[:, k:k + 1], None, ALU.mult)
                last.then_inc(f_wm.sem, 1)
                for i in range(NB + 2):
                    b = i - 1
                    if i < NB:
                        dve.wait_ge(f_tr.sem, i + 1)
                        stats(bank(0, 2).rearrange("p (j d) -> p j d", j=NT), 0)
                        dve.wait_ge(f_sd[0].sem, i + 1)
                        then(nc.vector.reciprocal(rs[0], sd[0]))
                        nc.vector.scalar_tensor_tensor(nb, ag[0][:, :, 0], -1.0, rs[0], ALU.mult, ALU.mult).then_inc(f_nb.sem, 1)
                    if i >= 2:
                        dve.wait_ge(f_sd[2].sem, i - 1)
                        then(nc.vector.reciprocal(rs[2], sd[2]))
                        if i >= 4:
                            dve.wait_ge(f_out[i % 2].sem, 16 * (i // 2 - 1))
                        norm(t3(rg), t3(yo[i % 2]), 2, f_n2)
                        dve.wait_ge(f_n2.sem, i - 1)
                    if 0 < i <= NB:
                        dve.wait_ge(f_v.sem, b + 1)
                        dve.wait_ge(f_sg.sem, b + 1)
                        nc.vector.tensor_tensor(rg[:], bank(4, 2), sg[:], ALU.mult).then_inc(f_rg.sem, 1)
                        dve.wait_ge(f_rg.sem, b + 1)
                        stats(t3(rg), 2)
                    if i < NB:
                        dve.wait_ge(f_r1.sem, i + 1)
                        stats(t3(x1[i % 3]), 1)
                        dve.wait_ge(f_sd[1].sem, i + 1)
                        then(nc.vector.reciprocal(rs[1], sd[1]))
                        if i:
                            dve.wait_ge(f_t1.sem, i)
                        norm(t3(x1[i % 3]), t3(n1), 1, f_n1)

            @block.scalar
            def _(act):
                def root(b, k):
                    act.wait_ge(f_st[k].sem, b + 1)
                    nc.scalar.activation(sd[k], ag[k][:, :, 1], ACT.Sqrt, bias=eps[:, 0:1]).then_inc(f_sd[k].sem, 1)

                for i in range(NB + 1):
                    b = i - 1
                    if i < NB:
                        root(i, 0)
                    if i < NB:
                        act.wait_ge(f_nb.sem, i + 1)
                        if i >= 3:
                            act.wait_ge(f_y.sem, i - 2)
                        for j in range(NT):
                            last = nc.scalar.activation(t3(x1[i % 3])[:, j, :], unit(ps, j), ACT.Identity,
                                                        bias=nb[:, j:j + 1], scale=rs[0][:, j:j + 1])
                        last.then_inc(f_n0.sem, 1)
                    if i:
                        act.wait_ge(f_k.sem, b + 1)
                        if b:
                            act.wait_ge(f_v.sem, b)
                        nc.scalar.activation(ka[:], bank(4, 2), ACT.Relu).then_inc(f_rl.sem, 1)
                        act.wait_ge(f_rl.sem, b + 1)
                        nc.scalar.activation(ka[:], ka[:], ACT.Square).then_inc(f_ka.sem, 1)
                        act.wait_ge(f_r.sem, b + 1)
                        if b:
                            act.wait_ge(f_rg.sem, b)
                        nc.scalar.activation(sg[:], bank(6, 2), ACT.Sigmoid).then_inc(f_sg.sem, 1)
                        root(b, 2)
                    if i < NB:
                        root(i, 1)
                        act.wait_ge(f_t1.sem, i + 1)
                        if i:
                            act.wait_ge(f_k.sem, i)
                            act.wait_ge(f_r.sem, i)
                        nc.scalar.activation(hx[:, 1:1 + T], bank(2, 2), ACT.Copy).then_inc(f_ev.sem, 1)

            @block.tensor
            def _(pe):
                pe.wait_ge(f_wm.sem, 1)
                pe.wait_ge(f_zc.sem, 1)
                for i in range(NB + 1):
                    b = i - 1
                    if i < NB:
                        if i:
                            pe.wait_ge(f_n0.sem, i)
                        for j in range(NT):
                            last = nc.tensor.transpose(unit(ps, j), accT3[:, i, j * P:(j + 1) * P], ident)
                        last.then_inc(f_tr.sem, 1)
                    if i:
                        pe.wait_ge(f_ev.sem, b + 1)
                        if b:
                            pe.wait_ge(f_rg.sem, b)
                            pe.wait_ge(f_sg.sem, b)
                        for k in range(2):
                            for q in range(2):
                                last = nc.tensor.matmul(bank(4 + k), wm[2 + q], hx[:, 1 - q + k * 512:1 - q + (k + 1) * 512],
                                                        start=(q == 0), stop=(q == 1))
                        last.then_inc(f_k.sem, 1)
                        for j in range(NT):
                            for q in range(2):
                                last = nc.tensor.matmul(unit(ps, 24 + j), hx[:, 1 - q + j * P:1 - q + (j + 1) * P], wm[q],
                                                        start=(q == 0), stop=(q == 1))
                        last.then_inc(f_r.sem, 1)
                        pe.wait_ge(f_ka.sem, b + 1)
                        for j in range(NT):
                            last = nc.tensor.matmul(unit(ps, 16 + j), unit(ka, j), wf_s[:, 2 * P:3 * P], start=True, stop=True)
                        last.then_inc(f_v.sem, 1)
                    if i < NB:
                        pe.wait_ge(f_n1.sem, i + 1)
                        if i:
                            pe.wait_ge(f_ev.sem, i)
                        for j in range(NT):
                            last = nc.tensor.transpose(unit(ps, 8 + j), unit(n1, j), ident)
                        last.then_inc(f_t1.sem, 1)


def kernel(L0_attn_x, L0_attn_Wq, L0_attn_Wk, L0_attn_Wv, L0_attn_Wb, L0_attn_Wa, L0_attn_A_log, L0_attn_dt_bias,
           L0_attn_Wo, L0_attn_conv_q, L0_attn_conv_k, L0_attn_conv_v, L0_ffn_W_r, L0_ffn_W_k, L0_ffn_W_v,
           L0_ffn_mu_r, L0_ffn_mu_k):
    import concourse.bacc as bacc
    from concourse.bass_utils import run_bass_kernel_spmd

    f = lambda a: np.asarray(a)
    wk = f(L0_attn_Wk).reshape(HP, P, D)
    wq = f(L0_attn_Wq).reshape(HP, P, D)
    wv = f(L0_attn_Wv).reshape(HP, 2, P, D)
    w = np.stack([wk, wq, wv[:, 0], wv[:, 1]], 1)
    w = w.transpose(3, 0, 1, 2).reshape(D, HP, 2, 2 * P)
    ck = f(L0_attn_conv_k).reshape(HP, P, TAPS)
    cq = f(L0_attn_conv_q).reshape(HP, P, TAPS)
    cvw = f(L0_attn_conv_v).reshape(HP, 2, P, TAPS)
    taps = np.stack([ck, cq, cvw[:, 0], cvw[:, 1]], 1).transpose(2, 0, 1, 3).reshape(P, HP, 2, 2 * TAPS)
    wtab = np.concatenate([w, taps], 3)
    wo = f(L0_attn_Wo).reshape(D, HP, 2, DV).transpose(3, 1, 2, 0).reshape(DV, HP, 2 * D)
    wa = f(L0_attn_Wa).reshape(HP, 2, D).transpose(2, 1, 0)
    wb = f(L0_attn_Wb).reshape(HP, 2, D).transpose(2, 1, 0)
    wab = np.concatenate([wa, wb], 2).reshape(D, 32)
    col = lambda a: np.repeat(f(a).reshape(HP, 2).T, C, axis=0)
    hcol = np.concatenate([col(L0_attn_dt_bias), col(L0_attn_A_log)], 1)
    wf = np.concatenate([f(L0_ffn_W_r).T, f(L0_ffn_W_k).T, f(L0_ffn_W_v).T], 1)
    mu = np.stack([f(L0_ffn_mu_r), f(L0_ffn_mu_k)], 1)
    arrays = {"x": f(L0_attn_x), "wtab": wtab, "wo": wo, "wab": wab, "hcol": hcol, "cst": constants(), "wf": wf, "mu": mu}
    arrays = {k: np.ascontiguousarray(v) for k, v in arrays.items()}
    nc = bacc.Bacc("TRN2", target_bir_lowering=False, num_devices=1)
    args = [nc.dram_tensor(k, v.shape, mybir.dt.from_np(v.dtype), kind="ExternalInput").ap() for k, v in arrays.items()]
    out = nc.dram_tensor("out", (NB, T, D), F32, kind="ExternalOutput").ap()
    build(nc, *args, out)
    r = run_bass_kernel_spmd(nc, [arrays], core_ids=[0])
    return r.results[0]["out"]
```
